# Optimizing a Trainium2 kernel written in Bass

```python
import numpy as np
import jax
import jax.numpy as jnp

def _softmax(x, axis=-1):
    return jax.nn.softmax(x, axis=axis)

def _gelu(x):
    return jax.nn.gelu(x, approximate=True)

def _silu(x):
    return jax.nn.silu(x)

def _sigmoid(x):
    return jax.nn.sigmoid(x)

def _layernorm(x, axis=-1, eps=1e-05):
    m = jnp.mean(x, axis=axis, keepdims=True)
    v = jnp.var(x, axis=axis, keepdims=True)
    return (x - m) / jnp.sqrt(v + eps)

def _scatter_add(tgt, idx, src, axis=0):
    return tgt.at[idx].add(src)

def _segment_sum(src, seg, n):
    return jax.ops.segment_sum(src, seg, n)
kernel_name = 'mk_dlrm_tower_d1_rec_r8_f79c23'

def setup_inputs(seed: int=0):
    np.random.seed(seed)
    _w = jnp.asarray

    def _rec_inputs():
        import jax
        import jax.numpy as jnp
        _tk = jax.random.key(seed)
        ids = jnp.stack([jax.random.randint(jax.random.fold_in(_tk, 200 + f), (2048,), 0, v, jnp.int32) for f, v in enumerate([1000, 12500, 1000, 125000, 1250, 1000, 12500, 12500, 1000, 1250, 1250, 1000, 1000, 1250, 12500, 1000, 12500, 1000, 12500, 12500, 1000, 1000, 1250, 1000, 1250, 1000])], axis=1)
        tbl_0 = 0.05 * jax.random.normal(jax.random.fold_in(_tk, 500 + 0), (1000, 128), jnp.float32)
        tbl_1 = 0.05 * jax.random.normal(jax.random.fold_in(_tk, 500 + 1), (12500, 128), jnp.float32)
        tbl_2 = 0.05 * jax.random.normal(jax.random.fold_in(_tk, 500 + 2), (1000, 128), jnp.float32)
        tbl_3 = 0.05 * jax.random.normal(jax.random.fold_in(_tk, 500 + 3), (125000, 128), jnp.float32)
        tbl_4 = 0.05 * jax.random.normal(jax.random.fold_in(_tk, 500 + 4), (1250, 128), jnp.float32)
        tbl_5 = 0.05 * jax.random.normal(jax.random.fold_in(_tk, 500 + 5), (1000, 128), jnp.float32)
        tbl_6 = 0.05 * jax.random.normal(jax.random.fold_in(_tk, 500 + 6), (12500, 128), jnp.float32)
        tbl_7 = 0.05 * jax.random.normal(jax.random.fold_in(_tk, 500 + 7), (12500, 128), jnp.float32)
        tbl_8 = 0.05 * jax.random.normal(jax.random.fold_in(_tk, 500 + 8), (1000, 128), jnp.float32)
        tbl_9 = 0.05 * jax.random.normal(jax.random.fold_in(_tk, 500 + 9), (1250, 128), jnp.float32)
        tbl_10 = 0.05 * jax.random.normal(jax.random.fold_in(_tk, 500 + 10), (1250, 128), jnp.float32)
        tbl_11 = 0.05 * jax.random.normal(jax.random.fold_in(_tk, 500 + 11), (1000, 128), jnp.float32)
        tbl_12 = 0.05 * jax.random.normal(jax.random.fold_in(_tk, 500 + 12), (1000, 128), jnp.float32)
        tbl_13 = 0.05 * jax.random.normal(jax.random.fold_in(_tk, 500 + 13), (1250, 128), jnp.float32)
        tbl_14 = 0.05 * jax.random.normal(jax.random.fold_in(_tk, 500 + 14), (12500, 128), jnp.float32)
        tbl_15 = 0.05 * jax.random.normal(jax.random.fold_in(_tk, 500 + 15), (1000, 128), jnp.float32)
        tbl_16 = 0.05 * jax.random.normal(jax.random.fold_in(_tk, 500 + 16), (12500, 128), jnp.float32)
        tbl_17 = 0.05 * jax.random.normal(jax.random.fold_in(_tk, 500 + 17), (1000, 128), jnp.float32)
        tbl_18 = 0.05 * jax.random.normal(jax.random.fold_in(_tk, 500 + 18), (12500, 128), jnp.float32)
        tbl_19 = 0.05 * jax.random.normal(jax.random.fold_in(_tk, 500 + 19), (12500, 128), jnp.float32)
        tbl_20 = 0.05 * jax.random.normal(jax.random.fold_in(_tk, 500 + 20), (1000, 128), jnp.float32)
        tbl_21 = 0.05 * jax.random.normal(jax.random.fold_in(_tk, 500 + 21), (1000, 128), jnp.float32)
        tbl_22 = 0.05 * jax.random.normal(jax.random.fold_in(_tk, 500 + 22), (1250, 128), jnp.float32)
        tbl_23 = 0.05 * jax.random.normal(jax.random.fold_in(_tk, 500 + 23), (1000, 128), jnp.float32)
        tbl_24 = 0.05 * jax.random.normal(jax.random.fold_in(_tk, 500 + 24), (1250, 128), jnp.float32)
        tbl_25 = 0.05 * jax.random.normal(jax.random.fold_in(_tk, 500 + 25), (1000, 128), jnp.float32)
        _rk = jax.random.fold_in(_tk, 7)
        r_dense_features = -0.000520686 + 1.00062 * jax.random.normal(jax.random.fold_in(_rk, 101), (2048, 128), jnp.float32)
        W_top1 = 0.0405887 * jax.random.normal(jax.random.fold_in(_tk, 801), (607, 512), jnp.float32)
        W_top2 = 0.0441942 * jax.random.normal(jax.random.fold_in(_tk, 802), (512, 256), jnp.float32)
        W_top3 = 0.0625 * jax.random.normal(jax.random.fold_in(_tk, 803), (256, 1), jnp.float32)
        b_top1 = jnp.zeros((512,), jnp.float32)
        b_top2 = jnp.zeros((256,), jnp.float32)
        return (r_dense_features, ids, tbl_0, tbl_1, tbl_2, tbl_3, tbl_4, tbl_5, tbl_6, tbl_7, tbl_8, tbl_9, tbl_10, tbl_11, tbl_12, tbl_13, tbl_14, tbl_15, tbl_16, tbl_17, tbl_18, tbl_19, tbl_20, tbl_21, tbl_22, tbl_23, tbl_24, tbl_25, W_top1, b_top1, W_top2, b_top2, W_top3)
    r_dense_features, ids, tbl_0, tbl_1, tbl_2, tbl_3, tbl_4, tbl_5, tbl_6, tbl_7, tbl_8, tbl_9, tbl_10, tbl_11, tbl_12, tbl_13, tbl_14, tbl_15, tbl_16, tbl_17, tbl_18, tbl_19, tbl_20, tbl_21, tbl_22, tbl_23, tbl_24, tbl_25, W_top1, b_top1, W_top2, b_top2, W_top3 = _rec_inputs()

    def _L0_rec_setup():
        import jax, jax.numpy as jnp
        import numpy as np
        NUM_SPARSE = 26
        EMBED_DIM = 128
        BATCH = 2048
        key = jax.random.key(seed)
        k1, k2 = jax.random.split(key)
        dense_features = jax.random.normal(k1, (BATCH, EMBED_DIM), dtype=jnp.float32)
        sparse_features = jax.random.normal(k2, (BATCH, NUM_SPARSE, EMBED_DIM), dtype=jnp.float32)
        return {'dense_features': dense_features, 'sparse_features': sparse_features}
    _L0_rec_all = _L0_rec_setup()
    _L0_rec_in = {k: v for k, v in _L0_rec_all.items() if k in ()}
    del _L0_rec_all
    return {'r_dense_features': r_dense_features, 'ids': ids, 'tbl_0': tbl_0, 'tbl_1': tbl_1, 'tbl_2': tbl_2, 'tbl_3': tbl_3, 'tbl_4': tbl_4, 'tbl_5': tbl_5, 'tbl_6': tbl_6, 'tbl_7': tbl_7, 'tbl_8': tbl_8, 'tbl_9': tbl_9, 'tbl_10': tbl_10, 'tbl_11': tbl_11, 'tbl_12': tbl_12, 'tbl_13': tbl_13, 'tbl_14': tbl_14, 'tbl_15': tbl_15, 'tbl_16': tbl_16, 'tbl_17': tbl_17, 'tbl_18': tbl_18, 'tbl_19': tbl_19, 'tbl_20': tbl_20, 'tbl_21': tbl_21, 'tbl_22': tbl_22, 'tbl_23': tbl_23, 'tbl_24': tbl_24, 'tbl_25': tbl_25, 'W_top1': W_top1, 'b_top1': b_top1, 'W_top2': W_top2, 'b_top2': b_top2, 'W_top3': W_top3}

def reference(r_dense_features, ids, tbl_0, tbl_1, tbl_2, tbl_3, tbl_4, tbl_5, tbl_6, tbl_7, tbl_8, tbl_9, tbl_10, tbl_11, tbl_12, tbl_13, tbl_14, tbl_15, tbl_16, tbl_17, tbl_18, tbl_19, tbl_20, tbl_21, tbl_22, tbl_23, tbl_24, tbl_25, W_top1, b_top1, W_top2, b_top2, W_top3):
    import jax
    import jax.numpy as jnp

    def _L0_rec_ref(dense_features, sparse_features):
        import jax, jax.numpy as jnp
        import numpy as np
        NUM_SPARSE = 26
        EMBED_DIM = 128
        BATCH = 2048
        F = NUM_SPARSE + 1
        combined = jnp.concatenate([dense_features[:, None, :], sparse_features], axis=1)
        interactions = jnp.einsum('bfd,bgd->bfg', combined, combined)
        iu, ju = jnp.triu_indices(F, k=1)
        interactions_flat = interactions[:, iu, ju]
        return jnp.concatenate([dense_features, interactions_flat], axis=1)
    e = jnp.stack([tbl_0[ids[:, 0]], tbl_1[ids[:, 1]], tbl_2[ids[:, 2]], tbl_3[ids[:, 3]], tbl_4[ids[:, 4]], tbl_5[ids[:, 5]], tbl_6[ids[:, 6]], tbl_7[ids[:, 7]], tbl_8[ids[:, 8]], tbl_9[ids[:, 9]], tbl_10[ids[:, 10]], tbl_11[ids[:, 11]], tbl_12[ids[:, 12]], tbl_13[ids[:, 13]], tbl_14[ids[:, 14]], tbl_15[ids[:, 15]], tbl_16[ids[:, 16]], tbl_17[ids[:, 17]], tbl_18[ids[:, 18]], tbl_19[ids[:, 19]], tbl_20[ids[:, 20]], tbl_21[ids[:, 21]], tbl_22[ids[:, 22]], tbl_23[ids[:, 23]], tbl_24[ids[:, 24]], tbl_25[ids[:, 25]]], axis=1)
    z = _L0_rec_ref(r_dense_features, e)
    z = z.reshape(z.shape[0], -1)
    h = jnp.concatenate([z, r_dense_features], axis=1)
    h = jnp.maximum(h @ W_top1 + b_top1, 0.0)
    h = jnp.maximum(h @ W_top2 + b_top2, 0.0)
    y = h @ W_top3
    return y

_drawn_inputs = setup_inputs


def setup_inputs(seed=0):
    import zlib

    import numpy as np

    out = dict(_drawn_inputs(seed))
    spreads = {'b_top1': (0.0, 0.1), 'b_top2': (0.0, 0.1)}
    factors = {}
    for name, (base, spread) in spreads.items():
        noise = np.random.default_rng([zlib.crc32(name.encode()), seed]).standard_normal(out[name].shape)
        drawn = base * np.exp(spread * noise) if base else spread * noise
        out[name] = jnp.asarray(drawn.astype(out[name].dtype))
    for name, factor in factors.items():
        out[name] = (out[name] * factor).astype(out[name].dtype)
    return out
```

```python
import numpy as np
import concourse.bass as bass
from concourse import mybir
from contextlib import ExitStack

BATCH, DIM, TABLES = 2048, 128, 26
VOCAB = [1000, 12500, 1000, 125000, 1250, 1000, 12500, 12500, 1000, 1250, 1250, 1000, 1000, 1250,
         12500, 1000, 12500, 1000, 12500, 12500, 1000, 1000, 1250, 1000, 1250, 1000]
FEATURES = TABLES + 1
PAIRS = FEATURES * (FEATURES - 1) // 2
HIDDEN1, HIDDEN2 = 512, 256

LOOKUPS = 10
LOOKED_UP = [t for t in range(TABLES) if VOCAB[t] == 1000][:LOOKUPS]
GATHERED = [t for t in range(TABLES) if t not in LOOKED_UP]
ORDER = [0] + [t + 1 for t in GATHERED] + [t + 1 for t in LOOKED_UP]


def pair_rows():
    rows = []
    for r in range(FEATURES):
        for s in range(r + 1, FEATURES):
            a, b = sorted((ORDER[r], ORDER[s]))
            rows.append(DIM + a * FEATURES - a * (a + 1) // 2 + (b - a - 1))
    return rows


def dlrm_tower(nc, dense, ids_gathered, ids_looked_up, tables, w1_dense, w1_pairs, b1, w2, b2, w3,
               out):
    fp32, fp32r, i32 = mybir.dt.float32, mybir.dt.float32r, mybir.dt.int32
    ALU, ACT = mybir.AluOpType, mybir.ActivationFunctionType

    TILE, TILES = 128, 4
    BLOCK = TILE * TILES
    BLOCKS = BATCH // BLOCK
    NG = len(GATHERED)
    ROWED = NG + 1
    PER_BANK = 4
    assert NG % PER_BANK == 0
    EMBED = [[0]] + [list(range(f, f + PER_BANK)) for f in range(1, ROWED, PER_BANK)]
    CHUNKS = 8
    TROWS = 1000 // CHUNKS
    SIDE = FEATURES - 1
    HALF = 16
    GRAMS = TILE // 4 // HALF * TILES
    TURNS = [list(range(r, min(r + 4, SIDE))) for r in range(0, SIDE, 4)]
    KCH = [128, 128, PAIRS - 256, DIM]
    N1, N2 = HIDDEN1 // 128, HIDDEN2 // 128
    ONE_HOTS = 4
    EMB_BANKS = LOOKUPS + TILES * len(EMBED)
    MIX_BANKS = len(TURNS) + len(KCH) + 1
    assert EMB_BANKS % 2 == 0 and MIX_BANKS % 2 == 0 and LOOKUPS % 2 == 0
    first_pair = [r * SIDE - r * (r - 1) // 2 for r in range(SIDE)]

    ctx = ExitStack()
    with ctx:
        def sb(name, shape, dt=fp32):
            return ctx.enter_context(nc.sbuf_tensor(name, shape, dt))

        def sem(name):
            return ctx.enter_context(nc.semaphore(name))

        def banks(name, n):
            return [ctx.enter_context(nc.psum_tensor(f"{name}{i}", [128, 512], fp32)) for i in range(n)]

        emb = sb("emb", [128, BLOCK, FEATURES])
        rows = sb("rows", [128, TILES, NG, DIM])
        dense_rows = sb("dense_rows", [128, TILES, DIM])
        gather_ids = sb("gather_ids", [128, TILES, NG], i32)
        gram = sb("gram", [128, SIDE, 128])
        pairs = sb("pairs", [128, 4, PAIRS])
        zh = sb("zh", [128, 4, BLOCK], fp32r)
        zl = sb("zl", [128, 4, BLOCK], fp32r)
        w1h = sb("w1h", [128, 4, HIDDEN1], fp32r)
        w1l = sb("w1l", [128, 4, HIDDEN1], fp32r)
        w2h = sb("w2h", [128, N1, HIDDEN2], fp32r)
        w2l = sb("w2l", [128, N1, HIDDEN2], fp32r)
        w3_sb = sb("w3_sb", [128, N2])
        b1_sb = sb("b1_sb", [128, N1])
        b2_sb = sb("b2_sb", [128, N2])
        h1_full = sb("h1_full", [128, 2, BLOCK])
        h1h = sb("h1h", [128, N1, BLOCK], fp32r)
        h1l = sb("h1l", [128, N1, BLOCK], fp32r)
        table = sb("table", [128, 2, CHUNKS * DIM])
        table_h = sb("table_h", [128, 2, CHUNKS * DIM], fp32r)
        table_l = sb("table_l", [128, 2, CHUNKS * DIM], fp32r)
        lookup_ids = sb("lookup_ids", [128, 2, BLOCK], i32)
        one_hot = sb("one_hot", [128, ONE_HOTS, BLOCK], fp32r)
        row_number = sb("row_number", [128, CHUNKS])
        row_number_i = sb("row_number_i", [128, CHUNKS], i32)
        ident = sb("ident", [128, 128])
        y_row = sb("y_row", [1, BLOCK])
        h2 = pairs[:, :, :].rearrange("p j n -> p (j n)")[:, 0:N2 * BLOCK].rearrange("p (c n) -> p c n", c=N2)
        w1_stage = gram[:, 0:20, :].rearrange("p a b -> p (a b)").rearrange("p (c n) -> p c n", n=HIDDEN1)
        w2_stage = h1_full[:, :, :].rearrange("p a b -> p (a b)").rearrange("p (c n) -> p c n", n=HIDDEN2)

        emb_ps = banks("emb_ps", 2)
        gram_ps = banks("gram_ps", 2)
        mix_ps = banks("mix_ps", 2)
        mlp_ps = banks("mlp_ps", 2)

        weights_in = sem("weights_in")
        w1_sum = sem("w1_sum")
        w_high = sem("w_high")
        w_low = sem("w_low")
        zeroed = sem("zeroed")
        const_ready = sem("const_ready")
        ids_in = [sem(f"ids_in{t}") for t in range(TILES)]
        rows_in = [[sem(f"rows_in{t}_{e}") for e in range(len(EMBED))] for t in range(TILES)]
        gathering = sem("gathering")
        dense_in = sem("dense_in")
        table_in = [sem(f"table_in{s}") for s in range(2)]
        lids_in = [sem(f"lids_in{s}") for s in range(2)]
        table_high = sem("table_high")
        table_low = sem("table_low")
        hot_ready = sem("hot_ready")
        hot_used = sem("hot_used")
        emb_full = sem("emb_full")
        emb_copied = sem("emb_copied")
        gram_full = sem("gram_full")
        gram_copied = sem("gram_copied")
        mix_full = sem("mix_full")
        mix_copied = sem("mix_copied")
        z_high = sem("z_high")
        mlp_full = sem("mlp_full")
        mlp_copied = sem("mlp_copied")
        h1_low = sem("h1_low")
        y_full = sem("y_full")
        y_out = sem("y_out")

        block = ctx.enter_context(nc.Block())

        def lookup_no(b, i):
            return b * LOOKUPS + i

        def lookup_bank(b, i):
            return b * EMB_BANKS + i

        def embed_bank(b, t, e):
            return b * EMB_BANKS + LOOKUPS + t * len(EMBED) + e

        LEAD = (["turn", 0], ["turn", 1], ["lookup", 0], ["turn", 2], ["turn", 3], ["lookup", 1],
                ["turn", 4], ["turn", 5], ["lookup", 2], ["turn", 6], ["z", 3], ["lookup", 3],
                ["z", 0], ["z", 1], ["z", 2], ["lookup", 4], ["layer1", 0], ["layer1", 1],
                ["lookup", 5], ["layer1", 2], ["layer1", 3], ["lookup", 6], ["layer2", 0],
                ["layer2", 1], ["lookup", 7], ["layer3", 0])
        TAIL = [tuple(s) for s in LEAD if s[0] != "lookup" or s[1] < LOOKUPS]
        TAIL += [("lookup", i) for i in range(8, LOOKUPS)]
        MIX_AT = {("turn", g): g for g in range(len(TURNS))}
        MIX_AT |= {("z", c): len(TURNS) + n for n, c in enumerate((3, 0, 1, 2))}
        MIX_AT |= {("layer3", 0): MIX_BANKS - 1}

        def tail(steps, b, ahead):
            for what, n in TAIL:
                if what == "lookup":
                    if ahead:
                        steps[what](b + 1, n)
                elif what in steps:
                    steps[what](b, n)

        def z_columns(ap):
            return ap.rearrange("p (n j) -> p j n", j=4)

        @block.sync
        def _(sp):
            def load_ids(start, t):
                tile_ids = ids_gathered[t * TILE:, :]
                sp.dma_start(gather_ids[:, t, :], tile_ids[bass.ds(start, TILE), :]) \
                    .then_inc(ids_in[t], 16)

            def load_dense(start):
                sp.dma_start(dense_rows[:, :, :],
                             dense[bass.ds(start, BLOCK), :].rearrange("(t p) d -> p t d", p=TILE)) \
                    .then_inc(dense_in, 16)

            def load_lookup(b, start, i, fresh=False):
                m = lookup_no(b, i)
                if not fresh:
                    sp.wait_ge(table_low, m - 1)
                sp.dma_start(table[0:TROWS, i % 2, :],
                             tables[LOOKED_UP[i]].rearrange("(p c) d -> p (c d)", c=CHUNKS)) \
                    .then_inc(table_in[i % 2], 16)
                if not fresh:
                    sp.wait_ge(hot_ready, CHUNKS * (m - 1))
                sp.dma_start(lookup_ids[:, i % 2, :],
                             ids_looked_up[i:i + 1, bass.ds(start, BLOCK)].to_broadcast([128, BLOCK])) \
                    .then_inc(lids_in[i % 2], 16)

            for t in range(TILES):
                load_ids(0, t)
            load_lookup(0, 0, 0, fresh=True)
            load_lookup(0, 0, 1, fresh=True)
            load_dense(0)
            sp.dma_start(w1_stage[:, 0, :], w1_pairs[0:128, :]).then_inc(weights_in, 16)
            sp.dma_start(w1_stage[:, 1, :], w1_pairs[128:256, :]).then_inc(weights_in, 16)
            sp.wait_ge(w1_sum, 1)
            sp.dma_start(w1_stage[0:KCH[2], 2, :], w1_pairs[256:PAIRS, :]).then_inc(weights_in, 16)
            sp.dma_start(w1_stage[:, 3, :], w1_dense[0:DIM, :]).then_inc(weights_in, 16)
            sp.dma_start(w1_stage[:, 4, :], w1_dense[DIM:2 * DIM, :]).then_inc(weights_in, 16)
            sp.dma_start(w2_stage, w2.rearrange("(c p) n -> p c n", p=128)).then_inc(weights_in, 16)
            sp.dma_start(w3_sb[:, :], w3).then_inc(weights_in, 16)
            sp.dma_start(b1_sb[:, :], b1).then_inc(weights_in, 16)
            sp.dma_start(b2_sb[:, :], b2).then_inc(weights_in, 16)
            for i in range(2, LOOKUPS):
                load_lookup(0, 0, i)
            with sp.Fori(0, BLOCKS - 1) as b:
                start = sp.snap((b + 1) * BLOCK)
                load_lookup(b + 1, start, 0)
                load_lookup(b + 1, start, 1)
                for t in range(TILES):
                    for e in range(1, len(EMBED)):
                        sp.wait_ge(rows_in[t][e], 16 * PER_BANK * (b + 1))
                    load_ids(start, t)
                for i in range(2, LOOKUPS):
                    load_lookup(b + 1, start, i)
                    if i == 5:
                        sp.wait_ge(mix_full, b * MIX_BANKS + MIX_AT["z", 3] + 1)
                        load_dense(start)

        @block.gpsimd
        def _(pool):
            pool.memset(ident[:, :], 0.0).then_inc(zeroed, 1)
            pool.iota(row_number_i[:, :], pattern=[[1, CHUNKS]], base=0, channel_multiplier=CHUNKS) \
                .then_inc(zeroed, 1)
            pool.wait_ge(zeroed, 2)
            pool.affine_select(out=ident[:, :], in_=ident[:, :], compare_op=ALU.not_equal, fill=1.0,
                               base=0, pattern=[[-1, 128]], channel_multiplier=1).then_inc(const_ready, 1)
            pool.tensor_copy(row_number[:, :], row_number_i[:, :]).then_inc(const_ready, 1)

            def gather(b, fresh=False):
                for t in range(TILES):
                    pool.wait_ge(ids_in[t], 16 * (b + 1))
                    if not fresh:
                        pool.wait_ge(emb_full, ((b - 1) * TILES + t + 1) * len(EMBED))
                        pool.sem_inc(gathering, 1)
                    for g in range(NG):
                        pool.indirect_dma_start(
                            out=rows[:, t, g, :], out_offset=None, in_=tables[GATHERED[g]],
                            in_offset=bass.IndirectOffsetOnAxis(ap=gather_ids[:, t, g:g + 1], axis=0),
                        ).then_inc(rows_in[t][1 + g // PER_BANK], 16)

            gather(0, fresh=True)
            with pool.Fori(1, BLOCKS) as b:
                gather(b)

        @block.tensor
        def _(pe):
            def embed(b, t):
                for e, features in enumerate(EMBED):
                    n = embed_bank(b, t, e)
                    if e == 0:
                        pe.wait_ge(dense_in, 16 * (b + 1))
                    else:
                        pe.wait_ge(rows_in[t][e], 16 * PER_BANK * (b + 1))
                    pe.wait_ge(emb_copied, n - 1)
                    bank = emb_ps[(LOOKUPS + t * len(EMBED) + e) % 2]
                    for k, f in enumerate(features):
                        src = rows[:, t, f - 1, :] if f > 0 else dense_rows[:, t, :]
                        last = pe.transpose(bank[:, 128 * k:128 * k + 128], src, ident[:, :])
                    last.then_inc(emb_full, 1)

            def grams(b, t):
                pe.wait_ge(emb_copied, embed_bank(b, t, len(EMBED) - 1) + 1)
                for h in range(2):
                    n = 2 * t + h
                    pe.wait_ge(gram_copied, b * GRAMS + n + 1)
                    for q in range(HALF):
                        for j in range(4):
                            s = t * TILE + 4 * (h * HALF + q) + j
                            last = pe.matmul(gram_ps[n % 2][32 * j:32 * j + SIDE, SIDE * q:SIDE * q + SIDE],
                                             emb[:, s, 1:FEATURES], emb[:, s, 0:SIDE], start=True, stop=True)
                    last.then_inc(gram_full, 1)

            def lookup(b, i, fresh=False):
                m = lookup_no(b, i)
                if not (fresh and i < 2):
                    pe.wait_ge(emb_copied, lookup_bank(b, i) - 1)
                pe.wait_ge(table_low, m + 1)
                for c in range(CHUNKS):
                    pe.wait_ge(hot_ready, CHUNKS * m + c + 1)
                    hot = one_hot[0:TROWS, c % ONE_HOTS, :]
                    pe.matmul(emb_ps[i % 2][:, :], table_h[0:TROWS, i % 2, DIM * c:DIM * c + DIM], hot,
                              start=(c == 0), stop=False)
                    last = pe.matmul(emb_ps[i % 2][:, :], table_l[0:TROWS, i % 2, DIM * c:DIM * c + DIM], hot,
                                     start=False, stop=(c == CHUNKS - 1))
                    last.then_inc(hot_used, 1)

            def mix(b, step):
                n = MIX_AT[step]
                pe.wait_ge(mix_copied, b * MIX_BANKS + n + 1)
                return mix_ps[n % 2]

            def turn(b, g):
                if g == 0:
                    pe.wait_ge(gram_copied, (b + 1) * GRAMS + 2)
                bank = mix(b, ("turn", g))
                for k, r in enumerate(TURNS[g]):
                    last = pe.transpose(bank[:, 128 * k:128 * k + 128], gram[:, r, :], ident[:, :])
                last.then_inc(mix_full, 1)

            def z(b, c):
                bank = mix(b, ("z", c))
                if c == 0:
                    pe.wait_ge(mix_copied, b * MIX_BANKS + len(TURNS) + 2)
                for j in range(4):
                    src = dense_rows[:, j, :] if c == 3 else pairs[:, j, 128 * c:128 * c + KCH[c]]
                    last = pe.transpose(bank[0:KCH[c], 128 * j:128 * j + 128], src, ident[:, :])
                last.then_inc(mix_full, 1)

            def layer1(b, n):
                if n == 0:
                    pe.wait_ge(mix_copied, b * MIX_BANKS + len(TURNS) + len(KCH) + 2)
                i = n
                pe.wait_ge(mlp_copied, b * (N1 + N2) + i + 1)
                order = (3, 0, 1, 2)
                for c in order:
                    k, cols = KCH[c], slice(128 * n, 128 * n + 128)
                    for w, x in ((w1h, zh), (w1h, zl), (w1l, zh)):
                        last = pe.matmul(mlp_ps[i % 2][:, :], w[0:k, c, cols], x[0:k, c, :],
                                         start=(c == 3 and w is w1h and x is zh), stop=(c == 2 and w is w1l))
                last.then_inc(mlp_full, 1)

            def layer2(b, n):
                if n == 0:
                    pe.wait_ge(h1_low, (b + 1) * N1)
                i = N1 + n
                pe.wait_ge(mlp_copied, b * (N1 + N2) + i + 1)
                for c in range(N1):
                    cols = slice(128 * n, 128 * n + 128)
                    for w, x in ((w2h, h1h), (w2h, h1l), (w2l, h1h)):
                        last = pe.matmul(mlp_ps[i % 2][:, :], w[:, c, cols], x[:, c, :],
                                         start=(c == 0 and w is w2h and x is h1h),
                                         stop=(c == N1 - 1 and w is w2l))
                last.then_inc(mlp_full, 1)

            def layer3(b, _):
                bank = mix(b, ("layer3", 0))
                pe.wait_ge(mlp_copied, (b + 1) * (N1 + N2) + 2)
                for c in range(N2):
                    last = pe.matmul(bank[0:1, :], w3_sb[:, c:c + 1], h2[:, c, :],
                                     start=(c == 0), stop=(c == N2 - 1))
                last.then_inc(mix_full, 1)

            def block_body(b, ahead):
                embed(b, 0)
                for t in range(TILES):
                    if t + 1 < TILES:
                        embed(b, t + 1)
                    grams(b, t)
                tail({"turn": turn, "z": z, "layer1": layer1, "layer2": layer2, "layer3": layer3,
                      "lookup": lookup}, b, ahead)

            pe.wait_ge(const_ready, 2)
            for i in range(LOOKUPS):
                lookup(0, i, fresh=True)
            pe.wait_ge(w_low, 2)
            with pe.Fori(0, BLOCKS - 1) as b:
                block_body(b, True)
            block_body(BLOCKS - 1, False)

        @block.scalar
        def _(act):
            def copy_embed(b, t):
                for e, features in enumerate(EMBED):
                    act.wait_ge(emb_full, (b * TILES + t) * len(EMBED) + e + 1)
                    bank = emb_ps[(LOOKUPS + t * len(EMBED) + e) % 2]
                    k = len(features)
                    act.activation(emb[:, t * TILE:(t + 1) * TILE, features[0]:features[0] + k],
                                   bank[:, 0:128 * k].rearrange("p (k s) -> p s k", k=k),
                                   ACT.Copy).then_inc(emb_copied, 1)

            def split_high(b, i, fresh=False):
                m = lookup_no(b, i)
                act.wait_ge(table_in[i % 2], 16 * (b * (LOOKUPS // 2) + i // 2 + 1))
                if not (fresh and i < 2):
                    act.wait_ge(hot_used, CHUNKS * (m - 1))
                act.activation(table_h[0:TROWS, i % 2, :], table[0:TROWS, i % 2, :], ACT.Copy) \
                    .then_inc(table_high, 1)

            def lookup(b, i):
                act.wait_ge(hot_used, CHUNKS * (lookup_no(b, i) + 1))
                act.activation(emb[:, :, ROWED + i], emb_ps[i % 2][:, :], ACT.Copy).then_inc(emb_copied, 1)
                if i + 2 < LOOKUPS:
                    split_high(b, i + 2)

            def z(b, c):
                n = MIX_AT["z", c]
                act.wait_ge(mix_full, b * MIX_BANKS + n + 1)
                k = KCH[c]
                src = mix_ps[n % 2][0:k, :]
                if c == 3:
                    act.activation(zh[0:k, c, :].rearrange("p (j n) -> p j n", j=4), z_columns(src),
                                   ACT.Copy).then_inc(z_high, 1)
                else:
                    act.activation(zh[0:k, c, :], src, ACT.Copy).then_inc(z_high, 1)

            def layer1(b, n):
                act.wait_ge(mlp_full, b * (N1 + N2) + n + 1)
                if n >= 2:
                    act.wait_ge(h1_low, b * N1 + n - 1)
                act.activation(h1_full[:, n % 2, :], mlp_ps[n % 2][:, :], ACT.Relu,
                               bias=b1_sb[:, n:n + 1])
                act.activation(h1h[:, n, :], mlp_ps[n % 2][:, :], ACT.Relu,
                               bias=b1_sb[:, n:n + 1]).then_inc(mlp_copied, 1)

            def layer2(b, n):
                i = N1 + n
                act.wait_ge(mlp_full, b * (N1 + N2) + i + 1)
                act.activation(h2[:, n, :], mlp_ps[i % 2][:, :], ACT.Relu,
                               bias=b2_sb[:, n:n + 1]).then_inc(mlp_copied, 1)

            def layer3(b, _):
                n = MIX_AT["layer3", 0]
                act.wait_ge(mix_full, b * MIX_BANKS + n + 1)
                act.wait_ge(y_out, 16 * (b + 1))
                act.activation(y_row[:, :].rearrange("o (n j) -> o j n", j=4),
                               mix_ps[n % 2][0:1, :].rearrange("o (j n) -> o j n", j=4),
                               ACT.Copy).then_inc(y_full, 1)
                act.wait_ge(y_full, b + 1)
                act.sem_inc(mix_copied, 1)
                act.dma_start(out[bass.ds(b * BLOCK, BLOCK), :].rearrange("s o -> o s"), y_row[:, :]) \
                    .then_inc(y_out, 16)

            def block_body(b, ahead):
                if ahead:
                    split_high(b + 1, 0)
                    split_high(b + 1, 1)
                for t in range(TILES):
                    copy_embed(b, t)
                tail({"z": z, "layer1": layer1, "layer2": layer2, "layer3": layer3,
                      "lookup": lookup}, b, ahead)

            act.sem_inc(mlp_copied, 2)
            act.sem_inc(y_out, 16)
            split_high(0, 0, fresh=True)
            split_high(0, 1, fresh=True)
            act.wait_ge(w1_sum, 2)
            act.wait_ge(weights_in, 16 * 9)
            act.activation(w1h[:, :, :], w1_stage[:, 0:4, :], ACT.Copy).then_inc(w_high, 1)
            act.activation(w2h[:, :, :], w2_stage, ACT.Copy).then_inc(w_high, 1)
            for i in range(LOOKUPS):
                lookup(0, i)
            with act.Fori(0, BLOCKS - 1) as b:
                block_body(b, True)
            block_body(BLOCKS - 1, False)
            act.wait_ge(y_out, 16 * (BLOCKS + 1))

        @block.vector
        def _(dve):
            def split_low(b, i, fresh=False):
                m = lookup_no(b, i)
                dve.wait_ge(table_high, m + 1)
                if not (fresh and i < 2):
                    dve.wait_ge(hot_used, CHUNKS * (m - 1))
                dve.tensor_tensor(table_l[0:TROWS, i % 2, :], table[0:TROWS, i % 2, :],
                                  table_h[0:TROWS, i % 2, :].bitcast(fp32), ALU.subtract) \
                    .then_inc(table_low, 1)

            def hots(b, i, half, fresh=False):
                m = lookup_no(b, i)
                if half == 0:
                    dve.wait_ge(lids_in[i % 2], 16 * (b * (LOOKUPS // 2) + i // 2 + 1))
                for c in range(half * ONE_HOTS, (half + 1) * ONE_HOTS):
                    if not (fresh and i == 0 and c < ONE_HOTS):
                        dve.wait_ge(hot_used, CHUNKS * m + c + 1 - ONE_HOTS)
                    dve.tensor_scalar(one_hot[0:TROWS, c % ONE_HOTS, :], lookup_ids[0:TROWS, i % 2, :],
                                      row_number[0:TROWS, c:c + 1], None, ALU.is_equal) \
                        .then_inc(hot_ready, 1)

            def lookup(b, i):
                hots(b, i, 1)
                if i + 1 < LOOKUPS:
                    hots(b, i + 1, 0)
                if i + 2 < LOOKUPS:
                    split_low(b, i + 2)

            def copy_gram(b, n):
                dve.wait_ge(gram_full, b * GRAMS + n + 1)
                dve.tensor_copy(gram[:, :, HALF * n:HALF * n + HALF].rearrange("p r q -> p q r"),
                                gram_ps[n % 2][:, 0:SIDE * HALF].rearrange("p (q r) -> p q r", r=SIDE)) \
                    .then_inc(gram_copied, 1)

            def turn(b, g):
                n = MIX_AT["turn", g]
                dve.wait_ge(mix_full, b * MIX_BANKS + n + 1)
                for k, r in enumerate(TURNS[g]):
                    src = mix_ps[n % 2][:, 128 * k:128 * k + 128].rearrange("p (j s) -> p j s", j=4)
                    last = dve.tensor_copy(pairs[:, :, first_pair[r]:first_pair[r] + SIDE - r],
                                           src[:, :, r:SIDE])
                last.then_inc(mix_copied, 1)

            def z(b, c):
                n = MIX_AT["z", c]
                dve.wait_ge(z_high, b * len(KCH) + n - len(TURNS) + 1)
                k = KCH[c]
                low, high, src = zl[0:k, c, :], zh[0:k, c, :].bitcast(fp32), mix_ps[n % 2][0:k, :]
                if c == 3:
                    low, high = (x.rearrange("p (j n) -> p j n", j=4) for x in (low, high))
                    src = z_columns(src)
                dve.tensor_tensor(low, src, high, ALU.subtract).then_inc(mix_copied, 1)

            def layer1(b, n):
                dve.wait_ge(mlp_copied, b * (N1 + N2) + n + 3)
                dve.tensor_tensor(h1l[:, n, :], h1_full[:, n % 2, :], h1h[:, n, :].bitcast(fp32),
                                  ALU.subtract).then_inc(h1_low, 1)

            def block_body(b, ahead):
                if ahead:
                    split_low(b + 1, 0)
                    split_low(b + 1, 1)
                    hots(b + 1, 0, 0)
                for n in range(GRAMS):
                    copy_gram(b, n)
                tail({"turn": turn, "z": z, "layer1": layer1, "lookup": lookup}, b, ahead)

            dve.memset(w1_stage[:, 2, :], 0.0).then_inc(w1_sum, 1)
            for bank in gram_ps:
                dve.memset(bank[:, :], 0.0).then_inc(gram_copied, 1)
            dve.sem_inc(mix_copied, 2)
            split_low(0, 0, fresh=True)
            split_low(0, 1, fresh=True)
            dve.wait_ge(const_ready, 2)
            hots(0, 0, 0, fresh=True)
            dve.wait_ge(weights_in, 16 * 9)
            dve.tensor_tensor(w1_stage[:, 3, :], w1_stage[:, 3, :], w1_stage[:, 4, :], ALU.add) \
                .then_inc(w1_sum, 1)
            dve.wait_ge(w_high, 2)
            dve.tensor_tensor(w1l[:, :, :], w1_stage[:, 0:4, :], w1h[:, :, :].bitcast(fp32), ALU.subtract) \
                .then_inc(w_low, 1)
            dve.tensor_tensor(w2l[:, :, :], w2_stage, w2h[:, :, :].bitcast(fp32), ALU.subtract) \
                .then_inc(w_low, 1)
            for i in range(LOOKUPS):
                lookup(0, i)
            with dve.Fori(0, BLOCKS - 1) as b:
                block_body(b, True)
            block_body(BLOCKS - 1, False)


def kernel(**inputs):
    import concourse.bacc as bacc
    from concourse.bass_utils import run_bass_kernel_spmd

    ids = np.asarray(inputs["ids"])
    w1 = np.asarray(inputs["W_top1"])
    arrays = {
        "dense": np.ascontiguousarray(inputs["r_dense_features"]),
        "ids_gathered": np.ascontiguousarray(ids[:, GATHERED]),
        "ids_looked_up": np.ascontiguousarray(ids[:, LOOKED_UP].T),
        "w1_dense": np.ascontiguousarray(np.concatenate([w1[:DIM], w1[DIM + PAIRS:]])),
        "w1_pairs": np.ascontiguousarray(w1[pair_rows()]),
        "b1": np.ascontiguousarray(np.asarray(inputs["b_top1"]).reshape(-1, 128).T),
        "w2": np.ascontiguousarray(inputs["W_top2"]),
        "b2": np.ascontiguousarray(np.asarray(inputs["b_top2"]).reshape(-1, 128).T),
        "w3": np.ascontiguousarray(np.asarray(inputs["W_top3"]).reshape(-1, 128).T),
    }
    for t in range(TABLES):
        arrays[f"table{t}"] = np.ascontiguousarray(inputs[f"tbl_{t}"])

    nc = bacc.Bacc("TRN2", target_bir_lowering=False, num_devices=1)
    ap = {name: nc.dram_tensor(name, a.shape, mybir.dt.from_np(a.dtype), kind="ExternalInput").ap()
          for name, a in arrays.items()}
    out = nc.dram_tensor("y", (BATCH, 1), mybir.dt.float32, kind="ExternalOutput").ap()
    dlrm_tower(nc, ap["dense"], ap["ids_gathered"], ap["ids_looked_up"],
               [ap[f"table{t}"] for t in range(TABLES)], ap["w1_dense"], ap["w1_pairs"],
               ap["b1"], ap["w2"], ap["b2"], ap["w3"], out)
    return run_bass_kernel_spmd(nc, [arrays], core_ids=[0]).results[0]["y"]
```

```python
import numpy as np
import concourse.bass as bass
from concourse import mybir
from contextlib import ExitStack

BATCH, DIM, TABLES = 2048, 128, 26
VOCAB = [1000, 12500, 1000, 125000, 1250, 1000, 12500, 12500, 1000, 1250, 1250, 1000, 1000, 1250,
         12500, 1000, 12500, 1000, 12500, 12500, 1000, 1000, 1250, 1000, 1250, 1000]
FEATURES = TABLES + 1
PAIRS = FEATURES * (FEATURES - 1) // 2
HIDDEN1, HIDDEN2 = 512, 256

LOOKUPS = 10
LOOKED_UP = [t for t in range(TABLES) if VOCAB[t] == 1000][:LOOKUPS]
GATHERED = [t for t in range(TABLES) if t not in LOOKED_UP]
ORDER = [0] + [t + 1 for t in GATHERED] + [t + 1 for t in LOOKED_UP]


def pair_rows():
    rows = []
    for r in range(FEATURES):
        for s in range(r + 1, FEATURES):
            a, b = sorted((ORDER[r], ORDER[s]))
            rows.append(DIM + a * FEATURES - a * (a + 1) // 2 + (b - a - 1))
    return rows


def dlrm_tower(nc, dense, ids_gathered, ids_looked_up, tables, w1_dense, w1_pairs, b1, w2, b2, w3,
               out):
    fp32, fp32r, i32 = mybir.dt.float32, mybir.dt.float32r, mybir.dt.int32
    ALU, ACT = mybir.AluOpType, mybir.ActivationFunctionType

    TILE, TILES = 128, 4
    BLOCK = TILE * TILES
    BLOCKS = BATCH // BLOCK
    NG = len(GATHERED)
    ROWED = NG + 1
    PER_BANK = 4
    assert NG % PER_BANK == 0
    EMBED = [[0]] + [list(range(f, f + PER_BANK)) for f in range(1, ROWED, PER_BANK)]
    CHUNKS = 8
    TROWS = 1000 // CHUNKS
    SIDE = FEATURES - 1
    HALF = 16
    GRAMS = TILE // 4 // HALF * TILES
    TURNS = [list(range(r, r + 4)) for r in range(0, 20, 4)] + [[20, 21], [22, 23], [24, 25]]
    KCH = [128, 128, PAIRS - 256, DIM]
    N1, N2 = HIDDEN1 // 128, HIDDEN2 // 128
    ONE_HOTS = 10
    assert LOOKUPS % 2 == 0

    halves = [("lookup", i, h) for i in range(LOOKUPS) for h in range(2)]
    embeds = [("embed", t, e) for t in range(TILES - 2) for e in range(len(EMBED))]
    own = [[("turn", 0), ("turn", 1)], [("turn", 2), ("turn", 3)], [("turn", 4), ("turn", 5)],
           [("turn", 6), ("turn", 7)], [("z", 3), ("z", 0)], [("z", 1), ("z", 2)], [],
           [("layer1", 0, 0)], [("layer1", 0, 1)], [("layer1", 1, 0), ("layer1", 1, 1)],
           [("layer1", 2, 0), ("layer1", 2, 1)], [("layer1", 3, 0), ("layer1", 3, 1)], "E",
           [("layer2", 0)], [("layer2", 1)], "E", [("layer3",)], "E", "E", "E", "E", "E", "E"]
    TAIL = []
    spaces = own.count("E")
    for k, steps in enumerate(own):
        if steps == "E":
            n = -(-len(embeds) // spaces)
            spaces, steps, embeds = spaces - 1, embeds[:n], embeds[n:]
        TAIL += steps
        upto = (k + 1) * 2 * LOOKUPS // len(own)
        if "E" in own[k + 1:k + 2]:
            upto += upto % 2
        TAIL += [s for s in halves[:upto] if s not in TAIL]
    assert len(TAIL) == len(set(TAIL))
    BODY = [("gram", 0), ("gram", 1)] + [("embed", 2, e) for e in range(len(EMBED))]
    BODY += [("gram", 2), ("gram", 3)] + [("embed", 3, e) for e in range(len(EMBED))]
    BODY += [("gram", n) for n in range(4, GRAMS)]

    EMB_USES = [s for s in TAIL + BODY if s[0] == "embed" or (s[0] == "lookup" and s[2] == 1)]
    MIX_USES = [("gram", n) for n in range(GRAMS)] + [s for s in TAIL if s[0] in ("turn", "z", "layer3")]
    assert len(EMB_USES) % 3 == 0 and len(MIX_USES) % 3 == 0

    def by_act(use):
        return use[0] in ("turn", "layer3")

    ACT_USES = [u for u in MIX_USES if by_act(u)]
    DVE_USES = [u for u in MIX_USES if not by_act(u)]

    first_pair = [r * SIDE - r * (r - 1) // 2 for r in range(SIDE)]

    ctx = ExitStack()
    with ctx:
        def sb(name, shape, dt=fp32):
            return ctx.enter_context(nc.sbuf_tensor(name, shape, dt))

        def sem(name):
            return ctx.enter_context(nc.semaphore(name))

        def banks(name, n):
            return [ctx.enter_context(nc.psum_tensor(f"{name}{i}", [128, 512], fp32)) for i in range(n)]

        emb = sb("emb", [128, BLOCK, FEATURES])
        rows = sb("rows", [128, TILES, NG, DIM])
        dense_rows = sb("dense_rows", [128, TILES, DIM])
        gather_ids = sb("gather_ids", [128, TILES, NG], i32)
        shared_at = nc.sbuf_base
        shared = sb("shared", [128, 2 * N1 * BLOCK])
        gram = nc.alloc_sbuf_tensor_at("gram", [128, SIDE, 128], fp32, offset=shared_at)
        h1h = nc.alloc_sbuf_tensor_at("h1h", [128, N1, BLOCK], fp32r, offset=shared_at)
        h1l = nc.alloc_sbuf_tensor_at("h1l", [128, N1, BLOCK], fp32r, offset=shared_at + N1 * BLOCK * 4)
        pairs = sb("pairs", [128, 4, PAIRS])
        zh = sb("zh", [128, 4, BLOCK], fp32r)
        zl = sb("zl", [128, 4, BLOCK], fp32r)
        w1h = sb("w1h", [128, 4, HIDDEN1], fp32r)
        w1l = sb("w1l", [128, 4, HIDDEN1], fp32r)
        w2h = sb("w2h", [128, N1, HIDDEN2], fp32r)
        w2l = sb("w2l", [128, N1, HIDDEN2], fp32r)
        w3_sb = sb("w3_sb", [128, N2])
        b1_sb = sb("b1_sb", [128, N1])
        b2_sb = sb("b2_sb", [128, N2])
        h1_full = sb("h1_full", [128, 2, BLOCK])
        table = sb("table", [128, 2, CHUNKS * DIM])
        table_h = sb("table_h", [128, 2, CHUNKS * DIM], fp32r)
        table_l = sb("table_l", [128, 2, CHUNKS * DIM], fp32r)
        lookup_ids = sb("lookup_ids", [128, 2, BLOCK], i32)
        one_hot = sb("one_hot", [128, ONE_HOTS, BLOCK], fp32r)
        row_number = sb("row_number", [128, CHUNKS])
        row_number_i = sb("row_number_i", [128, CHUNKS], i32)
        ident = sb("ident", [128, 128])
        y_rows = sb("y_rows", [128, TILE])
        h2 = pairs[:, :, :].rearrange("p j n -> p (j n)")[:, 0:N2 * BLOCK].rearrange("p (c n) -> p c n", c=N2)
        w1_stage = gram[:, 0:20, :].rearrange("p a b -> p (a b)").rearrange("p (c n) -> p c n", n=HIDDEN1)
        w2_stage = h1_full[:, :, :].rearrange("p a b -> p (a b)").rearrange("p (c n) -> p c n", n=HIDDEN2)

        emb_ps = banks("emb_ps", 3)
        mix_ps = banks("mix_ps", 3)
        mlp_ps = banks("mlp_ps", 2)

        weights_in = sem("weights_in")
        w1_sum = sem("w1_sum")
        w_high = sem("w_high")
        w_low = sem("w_low")
        zeroed = sem("zeroed")
        const_ready = sem("const_ready")
        ids_in = [sem(f"ids_in{t}") for t in range(TILES)]
        rows_in = [[sem(f"rows_in{t}_{e}") for e in range(len(EMBED))] for t in range(TILES)]
        gathering = sem("gathering")
        dense_in = sem("dense_in")
        table_in = [sem(f"table_in{s}") for s in range(2)]
        lids_in = [sem(f"lids_in{s}") for s in range(2)]
        table_high = sem("table_high")
        table_low = sem("table_low")
        hot_ready = sem("hot_ready")
        hot_used = sem("hot_used")
        emb_full = sem("emb_full")
        emb_copied = sem("emb_copied")
        mix_zeroed = sem("mix_zeroed")
        mix_full = sem("mix_full")
        mix_copied_act = sem("mix_copied_act")
        mix_copied_dve = sem("mix_copied_dve")
        z_high = sem("z_high")
        mlp_full = sem("mlp_full")
        mlp_copied = sem("mlp_copied")
        h1_low = sem("h1_low")
        y_full = sem("y_full")
        y_out = sem("y_out")

        block = ctx.enter_context(nc.Block())

        def wait(engine, semaphore, count):
            if not (isinstance(count, int) and count <= 0):
                engine.wait_ge(semaphore, count)

        def lookup_no(b, i):
            return b * LOOKUPS + i

        def hot_no(b, i, c):
            return lookup_no(b, i) * CHUNKS + c

        def hot_slot(i, c):
            return (i * CHUNKS + c) % ONE_HOTS

        def emb_no(b, use):
            return b * len(EMB_USES) + EMB_USES.index(use)

        def emb_bank(use):
            return emb_ps[EMB_USES.index(use) % 3]

        def mix_no(b, use):
            return b * len(MIX_USES) + MIX_USES.index(use)

        def mix_bank(use):
            return mix_ps[MIX_USES.index(use) % 3]

        def mix_done(b, use):
            if by_act(use):
                return mix_copied_act, (b + 1) * len(ACT_USES) + ACT_USES.index(use) + 1
            return mix_copied_dve, (b + 1) * len(DVE_USES) + DVE_USES.index(use) + 1

        def mix_before(b, use):
            n = MIX_USES.index(use) - 3
            return mix_done(b if n >= 0 else b - 1, MIX_USES[n])

        def run_tail(b, own, ahead):
            for what, *n in TAIL:
                if what in ahead and (isinstance(b, bass.RuntimeValue) or b < BLOCKS - 1):
                    ahead[what](b + 1, *n)
                if what in own and not (isinstance(b, int) and b < 0):
                    own[what](b, *n)

        def z_columns(ap):
            return ap.rearrange("p (n j) -> p j n", j=4)

        @block.sync
        def _(sp):
            def load_ids(start, t):
                tile_ids = ids_gathered[t * TILE:, :]
                sp.dma_start(gather_ids[:, t, :], tile_ids[bass.ds(start, TILE), :]) \
                    .then_inc(ids_in[t], 16)

            def load_dense(start):
                sp.dma_start(dense_rows[:, :, :],
                             dense[bass.ds(start, BLOCK), :].rearrange("(t p) d -> p t d", p=TILE)) \
                    .then_inc(dense_in, 16)

            def load_lookup(b, start, i):
                m = lookup_no(b, i)
                wait(sp, table_low, m - 1)
                sp.dma_start(table[0:TROWS, i % 2, :],
                             tables[LOOKED_UP[i]].rearrange("(p c) d -> p (c d)", c=CHUNKS)) \
                    .then_inc(table_in[i % 2], 16)
                wait(sp, hot_ready, CHUNKS * (m - 1))
                sp.dma_start(lookup_ids[:, i % 2, :],
                             ids_looked_up[i:i + 1, bass.ds(start, BLOCK)].to_broadcast([128, BLOCK])) \
                    .then_inc(lids_in[i % 2], 16)

            for t in range(TILES):
                load_ids(0, t)
            load_lookup(0, 0, 0)
            load_lookup(0, 0, 1)
            load_dense(0)
            sp.dma_start(w1_stage[:, 0, :], w1_pairs[0:128, :]).then_inc(weights_in, 16)
            sp.dma_start(w1_stage[:, 1, :], w1_pairs[128:256, :]).then_inc(weights_in, 16)
            sp.wait_ge(w1_sum, 1)
            sp.dma_start(w1_stage[0:KCH[2], 2, :], w1_pairs[256:PAIRS, :]).then_inc(weights_in, 16)
            sp.dma_start(w1_stage[:, 3, :], w1_dense[0:DIM, :]).then_inc(weights_in, 16)
            sp.dma_start(w1_stage[:, 4, :], w1_dense[DIM:2 * DIM, :]).then_inc(weights_in, 16)
            sp.dma_start(w2_stage, w2.rearrange("(c p) n -> p c n", p=128)).then_inc(weights_in, 16)
            sp.dma_start(w3_sb[:, :], w3).then_inc(weights_in, 16)
            sp.dma_start(b1_sb[:, :], b1).then_inc(weights_in, 16)
            sp.dma_start(b2_sb[:, :], b2).then_inc(weights_in, 16)
            for i in range(2, LOOKUPS):
                load_lookup(0, 0, i)
            with sp.Fori(0, BLOCKS - 1) as b:
                start = sp.snap((b + 1) * BLOCK)
                load_lookup(b + 1, start, 0)
                load_lookup(b + 1, start, 1)
                for t in range(TILES):
                    for e in range(1, len(EMBED)):
                        sp.wait_ge(rows_in[t][e], 16 * PER_BANK * (b + 1))
                    load_ids(start, t)
                for i in range(2, LOOKUPS):
                    load_lookup(b + 1, start, i)
                    if i == 3:
                        sp.wait_ge(mix_full, mix_no(b, ("z", 3)) + 1)
                        load_dense(start)

        @block.gpsimd
        def _(pool):
            pool.memset(ident[:, :], 0.0).then_inc(zeroed, 1)
            pool.iota(row_number_i[:, :], pattern=[[1, CHUNKS]], base=0, channel_multiplier=CHUNKS) \
                .then_inc(zeroed, 1)
            pool.wait_ge(zeroed, 2)
            pool.affine_select(out=ident[:, :], in_=ident[:, :], compare_op=ALU.not_equal, fill=1.0,
                               base=0, pattern=[[-1, 128]], channel_multiplier=1).then_inc(const_ready, 1)
            pool.tensor_copy(row_number[:, :], row_number_i[:, :]).then_inc(const_ready, 1)

            def gather(b, fresh=False):
                for t in range(TILES):
                    pool.wait_ge(ids_in[t], 16 * (b + 1))
                    if not fresh:
                        pool.wait_ge(emb_full, ((b - 1) * TILES + t + 1) * len(EMBED))
                        pool.sem_inc(gathering, 1)
                    for g in range(NG):
                        pool.indirect_dma_start(
                            out=rows[:, t, g, :], out_offset=None, in_=tables[GATHERED[g]],
                            in_offset=bass.IndirectOffsetOnAxis(ap=gather_ids[:, t, g:g + 1], axis=0),
                        ).then_inc(rows_in[t][1 + g // PER_BANK], 16)

            gather(0, fresh=True)
            with pool.Fori(1, BLOCKS) as b:
                gather(b)

        @block.tensor
        def _(pe):
            def embed(b, t, e):
                if e == 0:
                    pe.wait_ge(dense_in, 16 * (b + 1))
                else:
                    pe.wait_ge(rows_in[t][e], 16 * PER_BANK * (b + 1))
                wait(pe, emb_copied, emb_no(b, ("embed", t, e)) - 2)
                bank = emb_bank(("embed", t, e))
                for k, f in enumerate(EMBED[e]):
                    src = rows[:, t, f - 1, :] if f > 0 else dense_rows[:, t, :]
                    last = pe.transpose(bank[:, 128 * k:128 * k + 128], src, ident[:, :])
                last.then_inc(emb_full, 1)

            def lookup(b, i, h):
                use = ("lookup", i, 1)
                if h == 0:
                    wait(pe, emb_copied, emb_no(b, use) - 2)
                    pe.wait_ge(table_low, lookup_no(b, i) + 1)
                for c in range(h * CHUNKS // 2, (h + 1) * CHUNKS // 2):
                    pe.wait_ge(hot_ready, hot_no(b, i, c) + 1)
                    hot = one_hot[0:TROWS, hot_slot(i, c), :]
                    cols = slice(DIM * c, DIM * c + DIM)
                    pe.matmul(emb_bank(use)[:, :], table_h[0:TROWS, i % 2, cols], hot,
                              start=(c == 0), stop=False)
                    last = pe.matmul(emb_bank(use)[:, :], table_l[0:TROWS, i % 2, cols], hot,
                                     start=False, stop=(c == CHUNKS - 1))
                    last.then_inc(hot_used, 1)

            def grams(b, n):
                if n % 2 == 0:
                    need = [u for u in EMB_USES if u[0] == "lookup" or u[1] == n // 2]
                    pe.wait_ge(emb_copied, emb_no(b, need[-1]) + 1)
                pe.wait_ge(*mix_before(b, ("gram", n)))
                bank = mix_bank(("gram", n))
                for q in range(HALF):
                    for j in range(4):
                        s = 4 * (n * HALF + q) + j
                        last = pe.matmul(bank[32 * j:32 * j + SIDE, SIDE * q:SIDE * q + SIDE],
                                         emb[:, s, 1:FEATURES], emb[:, s, 0:SIDE], start=True, stop=True)
                last.then_inc(mix_full, 1)

            def turn(b, g):
                if g == 0:
                    pe.wait_ge(*mix_done(b, ("gram", GRAMS - 1)))
                pe.wait_ge(*mix_before(b, ("turn", g)))
                for k, r in enumerate(TURNS[g]):
                    last = pe.transpose(mix_bank(("turn", g))[:, 128 * k:128 * k + 128], gram[:, r, :],
                                        ident[:, :])
                last.then_inc(mix_full, 1)

            def z(b, c):
                if c == 0:
                    pe.wait_ge(*mix_done(b, ("turn", len(TURNS) - 1)))
                pe.wait_ge(*mix_before(b, ("z", c)))
                for j in range(4):
                    src = dense_rows[:, j, :] if c == 3 else pairs[:, j, 128 * c:128 * c + KCH[c]]
                    last = pe.transpose(mix_bank(("z", c))[0:KCH[c], 128 * j:128 * j + 128], src,
                                        ident[:, :])
                last.then_inc(mix_full, 1)

            def layer1(b, n, h):
                if h == 0:
                    pe.wait_ge(mlp_copied, b * (N1 + N2) + n + 1)
                for c in ((3, 0), (1, 2))[h]:
                    pe.wait_ge(*mix_done(b, ("z", c)))
                    k, cols = KCH[c], slice(128 * n, 128 * n + 128)
                    for w, x in ((w1h, zh), (w1h, zl), (w1l, zh)):
                        last = pe.matmul(mlp_ps[n % 2][:, :], w[0:k, c, cols], x[0:k, c, :],
                                         start=(c == 3 and w is w1h and x is zh), stop=(c == 2 and w is w1l))
                if h == 1:
                    last.then_inc(mlp_full, 1)

            def layer2(b, n):
                i = N1 + n
                pe.wait_ge(mlp_copied, b * (N1 + N2) + i + 1)
                for c in range(N1):
                    pe.wait_ge(h1_low, b * N1 + c + 1)
                    cols = slice(128 * n, 128 * n + 128)
                    for w, x in ((w2h, h1h), (w2h, h1l), (w2l, h1h)):
                        last = pe.matmul(mlp_ps[i % 2][:, :], w[:, c, cols], x[:, c, :],
                                         start=(c == 0 and w is w2h and x is h1h),
                                         stop=(c == N1 - 1 and w is w2l))
                last.then_inc(mlp_full, 1)

            def layer3(b):
                pe.wait_ge(*mix_before(b, ("layer3",)))
                pe.wait_ge(mlp_copied, (b + 1) * (N1 + N2) + 2)
                for c in range(N2):
                    for t in range(TILES):
                        moving = h2[:, c, :].rearrange("p (j t q) -> p t j q", j=4, t=TILES)[:, t]
                        last = pe.matmul(mix_bank(("layer3",))[32 * t:32 * t + 1, 0:TILE],
                                         w3_sb[:, c:c + 1], moving, start=(c == 0), stop=(c == N2 - 1))
                last.then_inc(mix_full, 1)

            def block_body(b):
                for what, *n in BODY:
                    {"gram": grams, "embed": embed}[what](b, *n)
                run_tail(b, {"turn": turn, "z": z, "layer1": layer1, "layer2": layer2, "layer3": layer3}, ahead)

            ahead = {"lookup": lookup, "embed": embed}
            pe.wait_ge(const_ready, 2)
            run_tail(-1, {}, ahead)
            pe.wait_ge(mix_zeroed, 3)
            pe.wait_ge(w_low, 2)
            with pe.Fori(0, BLOCKS - 1) as b:
                block_body(b)
            block_body(BLOCKS - 1)

        @block.scalar
        def _(act):
            def embed(b, t, e):
                act.wait_ge(emb_full, (b * TILES + t) * len(EMBED) + e + 1)
                k = len(EMBED[e])
                act.activation(emb[:, t * TILE:(t + 1) * TILE, EMBED[e][0]:EMBED[e][0] + k],
                               emb_bank(("embed", t, e))[:, 0:128 * k].rearrange("p (k s) -> p s k", k=k),
                               ACT.Copy).then_inc(emb_copied, 1)

            def split_high(b, i):
                act.wait_ge(table_in[i % 2], 16 * (b * (LOOKUPS // 2) + i // 2 + 1))
                wait(act, hot_used, CHUNKS * (lookup_no(b, i) - 1))
                act.activation(table_h[0:TROWS, i % 2, :], table[0:TROWS, i % 2, :], ACT.Copy) \
                    .then_inc(table_high, 1)

            def lookup(b, i, h):
                if h == 1:
                    act.wait_ge(hot_used, CHUNKS * (lookup_no(b, i) + 1))
                    act.activation(emb[:, :, ROWED + i], emb_bank(("lookup", i, 1))[:, :], ACT.Copy) \
                        .then_inc(emb_copied, 1)
                elif 0 < i < LOOKUPS - 1:
                    split_high(b, i + 1)

            def turn(b, g):
                act.wait_ge(mix_full, mix_no(b, ("turn", g)) + 1)
                for k, r in enumerate(TURNS[g]):
                    src = mix_bank(("turn", g))[:, 128 * k:128 * k + 128].rearrange("p (j s) -> p j s", j=4)
                    last = act.activation(pairs[:, :, first_pair[r]:first_pair[r] + SIDE - r],
                                          src[:, :, r:SIDE], ACT.Copy)
                last.then_inc(mix_copied_act, 1)

            def z(b, c):
                act.wait_ge(mix_full, mix_no(b, ("z", c)) + 1)
                k = KCH[c]
                src = mix_bank(("z", c))[0:k, :]
                if c == 3:
                    act.activation(zh[0:k, c, :].rearrange("p (j n) -> p j n", j=4), z_columns(src),
                                   ACT.Copy).then_inc(z_high, 1)
                else:
                    act.activation(zh[0:k, c, :], src, ACT.Copy).then_inc(z_high, 1)

            def layer1(b, n, h):
                if h == 1:
                    act.wait_ge(mlp_full, b * (N1 + N2) + n + 1)
                    if n >= 2:
                        act.wait_ge(h1_low, b * N1 + n - 1)
                    act.activation(h1_full[:, n % 2, :], mlp_ps[n % 2][:, :], ACT.Relu,
                                   bias=b1_sb[:, n:n + 1])
                    act.activation(h1h[:, n, :], mlp_ps[n % 2][:, :], ACT.Relu,
                                   bias=b1_sb[:, n:n + 1]).then_inc(mlp_copied, 1)

            def layer2(b, n):
                i = N1 + n
                act.wait_ge(mlp_full, b * (N1 + N2) + i + 1)
                act.activation(h2[:, n, :], mlp_ps[i % 2][:, :], ACT.Relu,
                               bias=b2_sb[:, n:n + 1]).then_inc(mlp_copied, 1)

            def layer3(b):
                act.wait_ge(mix_full, mix_no(b, ("layer3",)) + 1)
                act.wait_ge(y_out, 16 * (b + 1))
                act.activation(y_rows[:, :].rearrange("o (q j) -> o j q", j=4),
                               mix_bank(("layer3",))[:, 0:TILE].rearrange("o (j q) -> o j q", j=4),
                               ACT.Copy).then_inc(mix_copied_act, 1)
                act.wait_ge(*mix_done(b, ("layer3",)))
                act.dma_start(out[bass.ds(b * BLOCK, BLOCK), :].rearrange("(t s) o -> t (s o)", t=TILES),
                              y_rows[0:128:32, :]).then_inc(y_out, 16)

            def block_body(b):
                if not isinstance(b, int):
                    split_high(b + 1, 0)
                    split_high(b + 1, 1)
                for what, *n in BODY:
                    if what == "embed":
                        embed(b, *n)
                run_tail(b, {"turn": turn, "z": z, "layer1": layer1, "layer2": layer2, "layer3": layer3}, ahead)

            ahead = {"lookup": lookup, "embed": embed}
            act.sem_inc(mlp_copied, 2)
            act.sem_inc(y_out, 16)
            act.sem_inc(mix_copied_act, len(ACT_USES))
            split_high(0, 0)
            split_high(0, 1)
            run_tail(-1, {}, ahead)
            act.wait_ge(w1_sum, 2)
            act.activation(w1h[:, :, :], w1_stage[:, 0:4, :], ACT.Copy).then_inc(w_high, 1)
            act.activation(w2h[:, :, :], w2_stage, ACT.Copy).then_inc(w_high, 1)
            with act.Fori(0, BLOCKS - 1) as b:
                block_body(b)
            block_body(BLOCKS - 1)
            act.wait_ge(y_out, 16 * (BLOCKS + 1))

        @block.vector
        def _(dve):
            def split_low(b, i):
                dve.wait_ge(table_high, lookup_no(b, i) + 1)
                wait(dve, hot_used, CHUNKS * (lookup_no(b, i) - 1))
                dve.tensor_tensor(table_l[0:TROWS, i % 2, :], table[0:TROWS, i % 2, :],
                                  table_h[0:TROWS, i % 2, :].bitcast(fp32), ALU.subtract) \
                    .then_inc(table_low, 1)

            def hots(b, i, h):
                if h == 0:
                    dve.wait_ge(lids_in[i % 2], 16 * (b * (LOOKUPS // 2) + i // 2 + 1))
                for c in range(h * CHUNKS // 2, (h + 1) * CHUNKS // 2):
                    wait(dve, hot_used, hot_no(b, i, c) + 1 - ONE_HOTS)
                    dve.tensor_scalar(one_hot[0:TROWS, hot_slot(i, c), :], lookup_ids[0:TROWS, i % 2, :],
                                      row_number[0:TROWS, c:c + 1], None, ALU.is_equal) \
                        .then_inc(hot_ready, 1)

            def lookup(b, i, h):
                if h == 0 and 0 < i < LOOKUPS - 1:
                    split_low(b, i + 1)
                if i + 1 < LOOKUPS:
                    hots(b, i + 1, h)

            def grams(b, n):
                dve.wait_ge(mix_full, mix_no(b, ("gram", n)) + 1)
                dve.tensor_copy(gram[:, :, HALF * n:HALF * n + HALF].rearrange("p r q -> p q r"),
                                mix_bank(("gram", n))[:, 0:SIDE * HALF].rearrange("p (q r) -> p q r", r=SIDE)) \
                    .then_inc(mix_copied_dve, 1)

            def z(b, c):
                order = [u[1] for u in TAIL if u[0] == "z"]
                dve.wait_ge(z_high, b * len(KCH) + order.index(c) + 1)
                k = KCH[c]
                low, high, src = zl[0:k, c, :], zh[0:k, c, :].bitcast(fp32), mix_bank(("z", c))[0:k, :]
                if c == 3:
                    low, high = (x.rearrange("p (j n) -> p j n", j=4) for x in (low, high))
                    src = z_columns(src)
                dve.tensor_tensor(low, src, high, ALU.subtract).then_inc(mix_copied_dve, 1)

            def layer1(b, n, h):
                if h == 1:
                    dve.wait_ge(mlp_copied, b * (N1 + N2) + n + 3)
                    dve.tensor_tensor(h1l[:, n, :], h1_full[:, n % 2, :], h1h[:, n, :].bitcast(fp32),
                                      ALU.subtract).then_inc(h1_low, 1)

            def block_body(b):
                begin = {1: (split_low, 0), 2: (split_low, 1), 3: (hots, 0, 0), 4: (hots, 0, 1)}
                for n in range(GRAMS):
                    grams(b, n)
                    if n in begin and not isinstance(b, int):
                        step, *m = begin[n]
                        step(b + 1, *m)
                run_tail(b, {"z": z, "layer1": layer1}, {"lookup": lookup})

            dve.memset(w1_stage[:, 2, :], 0.0).then_inc(w1_sum, 1)
            for bank in mix_ps:
                dve.memset(bank[:, :], 0.0).then_inc(mix_zeroed, 1)
            dve.sem_inc(mix_copied_dve, len(DVE_USES))
            split_low(0, 0)
            split_low(0, 1)
            dve.wait_ge(const_ready, 2)
            hots(0, 0, 0)
            hots(0, 0, 1)
            run_tail(-1, {}, {"lookup": lookup})
            dve.wait_ge(weights_in, 16 * 9)
            dve.tensor_tensor(w1_stage[:, 3, :], w1_stage[:, 3, :], w1_stage[:, 4, :], ALU.add) \
                .then_inc(w1_sum, 1)
            dve.wait_ge(w_high, 2)
            dve.tensor_tensor(w1l[:, :, :], w1_stage[:, 0:4, :], w1h[:, :, :].bitcast(fp32), ALU.subtract) \
                .then_inc(w_low, 1)
            dve.tensor_tensor(w2l[:, :, :], w2_stage, w2h[:, :, :].bitcast(fp32), ALU.subtract) \
                .then_inc(w_low, 1)
            with dve.Fori(0, BLOCKS - 1) as b:
                block_body(b)
            block_body(BLOCKS - 1)


def kernel(**inputs):
    import concourse.bacc as bacc
    from concourse.bass_utils import run_bass_kernel_spmd

    ids = np.asarray(inputs["ids"])
    w1 = np.asarray(inputs["W_top1"])
    arrays = {
        "dense": np.ascontiguousarray(inputs["r_dense_features"]),
        "ids_gathered": np.ascontiguousarray(ids[:, GATHERED]),
        "ids_looked_up": np.ascontiguousarray(ids[:, LOOKED_UP].T),
        "w1_dense": np.ascontiguousarray(np.concatenate([w1[:DIM], w1[DIM + PAIRS:]])),
        "w1_pairs": np.ascontiguousarray(w1[pair_rows()]),
        "b1": np.ascontiguousarray(np.asarray(inputs["b_top1"]).reshape(-1, 128).T),
        "w2": np.ascontiguousarray(inputs["W_top2"]),
        "b2": np.ascontiguousarray(np.asarray(inputs["b_top2"]).reshape(-1, 128).T),
        "w3": np.ascontiguousarray(np.asarray(inputs["W_top3"]).reshape(-1, 128).T),
    }
    for t in range(TABLES):
        arrays[f"table{t}"] = np.ascontiguousarray(inputs[f"tbl_{t}"])

    nc = bacc.Bacc("TRN2", target_bir_lowering=False, num_devices=1)
    ap = {name: nc.dram_tensor(name, a.shape, mybir.dt.from_np(a.dtype), kind="ExternalInput").ap()
          for name, a in arrays.items()}
    out = nc.dram_tensor("y", (BATCH, 1), mybir.dt.float32, kind="ExternalOutput").ap()
    dlrm_tower(nc, ap["dense"], ap["ids_gathered"], ap["ids_looked_up"],
               [ap[f"table{t}"] for t in range(TABLES)], ap["w1_dense"], ap["w1_pairs"],
               ap["b1"], ap["w2"], ap["b2"], ap["w3"], out)
    return run_bass_kernel_spmd(nc, [arrays], core_ids=[0]).results[0]["y"]
```

```python
import numpy as np
import concourse.bass as bass
from concourse import mybir
from contextlib import ExitStack

BATCH, DIM, TABLES = 2048, 128, 26
VOCAB = [1000, 12500, 1000, 125000, 1250, 1000, 12500, 12500, 1000, 1250, 1250, 1000, 1000, 1250,
         12500, 1000, 12500, 1000, 12500, 12500, 1000, 1000, 1250, 1000, 1250, 1000]
FEATURES = TABLES + 1
PAIRS = FEATURES * (FEATURES - 1) // 2
HIDDEN1, HIDDEN2 = 512, 256

LOOKUPS = 9
LOOKED_UP = [t for t in range(TABLES) if VOCAB[t] == 1000][:LOOKUPS]
GATHERED = [t for t in range(TABLES) if t not in LOOKED_UP]
ORDER = [0] + [t + 1 for t in GATHERED] + [t + 1 for t in LOOKED_UP]


def pair_rows():
    rows = []
    for r in range(FEATURES):
        for s in range(r + 1, FEATURES):
            a, b = sorted((ORDER[r], ORDER[s]))
            rows.append(DIM + a * FEATURES - a * (a + 1) // 2 + (b - a - 1))
    return rows


def dlrm_tower(nc, dense, ids_gathered, ids_looked_up, tables, w1_dense, w1_pairs, b1, w2, b2, w3,
               out):
    fp32, fp32r = mybir.dt.float32, mybir.dt.float32r
    i32, u32 = mybir.dt.int32, mybir.dt.uint32
    ALU, ACT = mybir.AluOpType, mybir.ActivationFunctionType

    TILE, TILES = 128, 4
    BLOCK = TILE * TILES
    BLOCKS = BATCH // BLOCK
    NG = len(GATHERED)
    ROWED = NG + 1
    EMBED = [list(range(f, min(f + 4, ROWED))) for f in range(0, ROWED, 4)]
    bank_of = {f: e for e, features in enumerate(EMBED) for f in features}
    CHUNKS = 8
    TROWS = 1000 // CHUNKS
    SIDE = FEATURES - 1
    HALF = 16
    GRAMS = TILE // 4 // HALF * TILES
    KCH = [128, 128, PAIRS - 256, DIM]
    N1, N2 = HIDDEN1 // 128, HIDDEN2 // 128
    ONE_HOTS = 9
    assert LOOKUPS * CHUNKS % ONE_HOTS == 0

    EARLY = 2
    lookups = [("lookup", i, h) for i in range(LOOKUPS) for h in range(2)]
    early, halves = lookups[:2 * EARLY], lookups[2 * EARLY:]
    embeds = [("embed", t, e) for t in range(TILES - 2) for e in range(len(EMBED))]
    PARTS = ((3,), (0,), (1, 2))
    LAST = len(PARTS) - 1
    own = [[("layer1", 0, 0)], [("layer1", 1, 0), ("z", 0, 0), ("z", 1, 0), ("z", 2, 0)],
           [("z", 0, 1), ("z", 1, 1)], [("z", 2, 1)],
           [("layer1", 0, 1)], [("layer1", 1, 1)], [("layer1", 0, 2)], [("layer1", 1, 2)],
           [("layer1", 2, p) for p in range(3)], [("layer1", 3, p) for p in range(3)], "E",
           [("layer2", 0)], [("layer2", 1)], "E", [("layer3",)], "E", "E", "E", "E", "E", "E"]
    TAIL = [("place", i) for i in range(EARLY)] + [("pair", 1)] + halves[:1]
    spaces = own.count("E")
    for k, steps in enumerate(own):
        if steps == "E":
            n = len(embeds) // spaces
            spaces, steps, embeds = spaces - 1, embeds[:n], embeds[n:]
        TAIL += steps
        upto = -(-(k + 1) * len(halves) // len(own))
        if "E" in own[k + 1:k + 2]:
            upto += upto % 2
        TAIL += [s for s in halves[:upto] if s not in TAIL]
    assert len(TAIL) == len(set(TAIL))
    tile2, tile3 = ([("embed", t, e) for e in range(len(EMBED))] for t in (2, 3))
    BODY = [("gram", 0), ("gram", 1), ("gram", 2), *tile2, ("gram", 3), ("gram", 4),
            *early, *tile3[:-1], ("dense",), ("gram", 5, 0), tile3[-1], ("gram", 5, 1),
            ("split", EARLY + 1), ("pair", 0), ("gram", 6), ("gram", 7)]

    EMB_USES = [s for s in TAIL + BODY if s[0] == "embed" or (s in halves and s[2] == 1)]
    MIX_USES = [("gram", n) for n in range(GRAMS)] + [("z", 0), ("z", 1), ("z", 2), ("none",)]
    MLP_USES = [("place", i) for i in range(EARLY)] + [("layer1", n) for n in range(N1)] + \
        [("layer2", n) for n in range(N2)] + [("layer3",), ("none",)]
    assert len(MLP_USES) % 2 == 0
    assert len(EMB_USES) % 3 == 0 and len(MIX_USES) % 3 == 0

    PAIR_TILES = [slice(0, TILES - 1), slice(TILES - 1, TILES)]
    PAIR_ACT = 11
    first_pair = [r * SIDE - r * (r - 1) // 2 for r in range(SIDE)]

    ctx = ExitStack()
    with ctx:
        def sb(name, shape, dt=fp32):
            return ctx.enter_context(nc.sbuf_tensor(name, shape, dt))

        def sem(name):
            return ctx.enter_context(nc.semaphore(name))

        def banks(name, n):
            return [ctx.enter_context(nc.psum_tensor(f"{name}{i}", [128, 512], fp32)) for i in range(n)]

        emb = sb("emb", [128, BLOCK, FEATURES])
        shared_at = nc.sbuf_base
        sb("shared", [128, 2 * N1 * BLOCK])
        gram = nc.alloc_sbuf_tensor_at("gram", [128, SIDE, 128], fp32, offset=shared_at)
        h1h = nc.alloc_sbuf_tensor_at("h1h", [128, N1, BLOCK], fp32r, offset=shared_at)
        h1l = nc.alloc_sbuf_tensor_at("h1l", [128, N1, BLOCK], fp32r, offset=shared_at + N1 * BLOCK * 4)
        rows = sb("rows", [128, TILES, NG, DIM])
        dense_rows = sb("dense_rows", [128, TILES, DIM])
        shared_z_at = nc.sbuf_base
        sb("shared_z", [128, TILES * SIDE * 32])
        turned = nc.alloc_sbuf_tensor_at("turned", [128, TILES, SIDE, 32], u32, offset=shared_z_at)
        zh = nc.alloc_sbuf_tensor_at("zh", [128, 3, BLOCK], fp32r, offset=shared_z_at)
        zl = nc.alloc_sbuf_tensor_at("zl", [128, 3, BLOCK], fp32r, offset=shared_z_at + 3 * BLOCK * 4)
        dense_h = sb("dense_h", [128, BLOCK], fp32r)
        dense_l = sb("dense_l", [128, BLOCK], fp32r)
        pairs = sb("pairs", [128, 4, PAIRS])
        gather_ids = sb("gather_ids", [128, TILES, NG], i32)
        w1h = sb("w1h", [128, 4, HIDDEN1], fp32r)
        w1l = sb("w1l", [128, 4, HIDDEN1], fp32r)
        w2h = sb("w2h", [128, N1, HIDDEN2], fp32r)
        w2l = sb("w2l", [128, N1, HIDDEN2], fp32r)
        w3_sb = sb("w3_sb", [128, N2])
        b1_sb = sb("b1_sb", [128, N1])
        b2_sb = sb("b2_sb", [128, N2])
        h1_full = sb("h1_full", [128, 2, BLOCK])
        table = sb("table", [128, 2, CHUNKS * DIM])
        table_h = sb("table_h", [128, 2, CHUNKS * DIM], fp32r)
        table_l = sb("table_l", [128, 2, CHUNKS * DIM], fp32r)
        lookup_ids = sb("lookup_ids", [128, 2, BLOCK], i32)
        one_hot = sb("one_hot", [128, ONE_HOTS, BLOCK], fp32r)
        row_number = sb("row_number", [128, CHUNKS])
        row_number_i = sb("row_number_i", [128, CHUNKS], i32)
        ident = sb("ident", [128, 128])
        y_rows = sb("y_rows", [128, TILE])
        h2 = pairs[:, :, :].rearrange("p j n -> p (j n)")[:, 0:N2 * BLOCK].rearrange("p (c n) -> p c n", c=N2)
        w1_stage = gram[:, 0:20, :].rearrange("p a b -> p (a b)").rearrange("p (c n) -> p c n", n=HIDDEN1)
        w2_stage = h1_full[:, :, :].rearrange("p a b -> p (a b)").rearrange("p (c n) -> p c n", n=HIDDEN2)

        emb_ps = banks("emb_ps", 3)
        mix_ps = banks("mix_ps", 3)
        mlp_ps = banks("mlp_ps", 2)

        weights_in = sem("weights_in")
        w1_sum = sem("w1_sum")
        w_high = sem("w_high")
        w_low = sem("w_low")
        zeroed = sem("zeroed")
        const_ready = sem("const_ready")
        ids_in = [sem(f"ids_in{t}") for t in range(TILES)]
        rows_in = [[sem(f"rows_in{t}_{e}") for e in range(len(EMBED))] for t in range(TILES)]
        gathering = sem("gathering")
        dense_in = sem("dense_in")
        table_in = [sem(f"table_in{s}") for s in range(2)]
        lids_in = [sem(f"lids_in{s}") for s in range(2)]
        table_high = sem("table_high")
        table_low = sem("table_low")
        hot_ready = sem("hot_ready")
        hot_used = sem("hot_used")
        emb_full = sem("emb_full")
        emb_copied = sem("emb_copied")
        mix_zeroed = sem("mix_zeroed")
        mix_full = sem("mix_full")
        mix_copied = sem("mix_copied")
        turn_done = sem("turn_done")
        first_pairs_done = sem("first_pairs_done")
        pairs_done = sem("pairs_done")
        dense_high = sem("dense_high")
        dense_low = sem("dense_low")
        z_high = sem("z_high")
        mlp_full = sem("mlp_full")
        mlp_copied = sem("mlp_copied")
        h1_low = sem("h1_low")
        y_full = sem("y_full")
        y_out = sem("y_out")

        block = ctx.enter_context(nc.Block())

        def wait(engine, semaphore, count):
            if not (isinstance(count, int) and count <= 0):
                engine.wait_ge(semaphore, count)

        def lookup_no(b, i):
            return b * LOOKUPS + i

        def slot_uses(b, i):
            return b * len(range(i % 2, LOOKUPS, 2)) + i // 2 + 1

        def slot_before(b, i):
            return lookup_no(b, i - 2) if i >= 2 else lookup_no(b - 1, range(i, LOOKUPS, 2)[-1])

        def gathered_in(e):
            return len([f for f in EMBED[e] if f > 0])

        def hot_no(b, i, c):
            return lookup_no(b, i) * CHUNKS + c

        def hot_slot(i, c):
            return (i * CHUNKS + c) % ONE_HOTS

        def emb_no(b, use):
            return b * len(EMB_USES) + EMB_USES.index(use)

        def emb_bank(use):
            return emb_ps[EMB_USES.index(use) % 3]

        def mlp_bank(use):
            return mlp_ps[MLP_USES.index(use) % 2]

        def mlp_no(b, use):
            return (b if use[0] == "place" else b + 1) * len(MLP_USES) + MLP_USES.index(use)

        def mlp_done(b, use):
            return mlp_copied, mlp_no(b, use) + 3

        def mlp_before(b, use):
            return mlp_copied, mlp_no(b, use) + 1

        def mix_no(b, use):
            return b * len(MIX_USES) + MIX_USES.index(use)

        def mix_bank(use):
            return mix_ps[MIX_USES.index(use) % 3]

        def mix_done(b, use):
            return mix_copied, mix_no(b + 1, use) + 1

        def mix_before(b, use):
            n = MIX_USES.index(use) - 3
            return mix_done(b if n >= 0 else b - 1, MIX_USES[n])

        def run(steps, b, own, ahead):
            for what, *n in steps:
                if what in ahead and (isinstance(b, bass.RuntimeValue) or b < BLOCKS - 1):
                    ahead[what](b + 1, *n)
                if what in own and not (isinstance(b, int) and b < 0):
                    own[what](b, *n)

        def dense_columns():
            return emb[:, :, 0].rearrange("p (t q j) -> p t j q", t=TILES, j=4)

        def as_dense(ap):
            return ap.rearrange("p (t j q) -> p t j q", t=TILES, j=4)

        def z_no(b, c):
            return b * 3 + c

        def input_done(b, c):
            if c == 3:
                return (dense_high, b + 1), (dense_low, b + 1)
            return (z_high, z_no(b, c) + 1), mix_done(b, ("z", c))

        def z_parts(c):
            if c == 3:
                return dense_h[:, :], dense_l[:, :]
            return zh[0:KCH[c], c, :], zl[0:KCH[c], c, :]

        @block.sync
        def _(sp):
            def load_ids(start, t):
                tile_ids = ids_gathered[t * TILE:, :]
                sp.dma_start(gather_ids[:, t, :], tile_ids[bass.ds(start, TILE), :]) \
                    .then_inc(ids_in[t], 16)

            def load_dense(start):
                sp.dma_start(dense_rows[:, :, :],
                             dense[bass.ds(start, BLOCK), :].rearrange("(t p) d -> p t d", p=TILE)) \
                    .then_inc(dense_in, 16)

            def load_lookup(b, start, i):
                wait(sp, table_low, slot_before(b, i) + 1)
                sp.dma_start(table[0:TROWS, i % 2, :],
                             tables[LOOKED_UP[i]].rearrange("(p c) d -> p (c d)", c=CHUNKS)) \
                    .then_inc(table_in[i % 2], 16)
                wait(sp, hot_ready, CHUNKS * (slot_before(b, i) + 1))
                sp.dma_start(lookup_ids[:, i % 2, :],
                             ids_looked_up[i:i + 1, bass.ds(start, BLOCK)].to_broadcast([128, BLOCK])) \
                    .then_inc(lids_in[i % 2], 16)

            load_ids(0, 0)
            load_lookup(0, 0, 0)
            load_ids(0, 1)
            load_lookup(0, 0, 1)
            for t in range(2, TILES):
                load_ids(0, t)
            load_dense(0)
            for i in range(2, 7):
                load_lookup(0, 0, i)
            sp.dma_start(w1_stage[:, 0, :], w1_pairs[0:128, :]).then_inc(weights_in, 16)
            sp.dma_start(w1_stage[:, 1, :], w1_pairs[128:256, :]).then_inc(weights_in, 16)
            sp.wait_ge(w1_sum, 1)
            sp.dma_start(w1_stage[0:KCH[2], 2, :], w1_pairs[256:PAIRS, :]).then_inc(weights_in, 16)
            sp.dma_start(w1_stage[:, 3, :], w1_dense[0:DIM, :]).then_inc(weights_in, 16)
            sp.dma_start(w1_stage[:, 4, :], w1_dense[DIM:2 * DIM, :]).then_inc(weights_in, 16)
            sp.dma_start(w2_stage, w2.rearrange("(c p) n -> p c n", p=128)).then_inc(weights_in, 16)
            sp.dma_start(w3_sb[:, :], w3).then_inc(weights_in, 16)
            sp.dma_start(b1_sb[:, :], b1).then_inc(weights_in, 16)
            sp.dma_start(b2_sb[:, :], b2).then_inc(weights_in, 16)
            for i in range(7, LOOKUPS):
                load_lookup(0, 0, i)
            with sp.Fori(0, BLOCKS - 1) as b:
                start = sp.snap((b + 1) * BLOCK)
                load_lookup(b + 1, start, 0)
                load_lookup(b + 1, start, 1)
                for t in range(TILES):
                    if t == TILES - 1:
                        load_lookup(b + 1, start, 2)
                        load_lookup(b + 1, start, 3)
                    sp.wait_ge(emb_full, (b * TILES + t + 1) * len(EMBED))
                    load_ids(start, t)
                for i in range(4, LOOKUPS):
                    load_lookup(b + 1, start, i)
                    if i == 5:
                        sp.wait_ge(emb_full, (b + 1) * TILES * len(EMBED))
                        load_dense(start)

        @block.gpsimd
        def _(pool):
            pool.memset(ident[:, :], 0.0).then_inc(zeroed, 1)
            pool.iota(row_number_i[:, :], pattern=[[1, CHUNKS]], base=0, channel_multiplier=CHUNKS) \
                .then_inc(zeroed, 1)
            pool.wait_ge(zeroed, 2)
            pool.affine_select(out=ident[:, :], in_=ident[:, :], compare_op=ALU.not_equal, fill=1.0,
                               base=0, pattern=[[-1, 128]], channel_multiplier=1).then_inc(const_ready, 1)
            pool.tensor_copy(row_number[:, :], row_number_i[:, :]).then_inc(const_ready, 1)

            def gather(b, fresh=False):
                for t in range(TILES):
                    pool.wait_ge(ids_in[t], 16 * (b + 1))
                    if not fresh:
                        pool.wait_ge(emb_full, ((b - 1) * TILES + t + 1) * len(EMBED))
                        pool.sem_inc(gathering, 1)
                    for g in range(NG):
                        pool.indirect_dma_start(
                            out=rows[:, t, g, :], out_offset=None, in_=tables[GATHERED[g]],
                            in_offset=bass.IndirectOffsetOnAxis(ap=gather_ids[:, t, g:g + 1], axis=0),
                        ).then_inc(rows_in[t][bank_of[g + 1]], 16)

            gather(0, fresh=True)
            with pool.Fori(1, BLOCKS) as b:
                gather(b)

        @block.tensor
        def _(pe):
            def embed(b, t, e):
                if e == 0:
                    pe.wait_ge(dense_in, 16 * (b + 1))
                pe.wait_ge(rows_in[t][e], 16 * gathered_in(e) * (b + 1))
                wait(pe, emb_copied, emb_no(b, ("embed", t, e)) - 2)
                bank = emb_bank(("embed", t, e))
                for k, f in enumerate(EMBED[e]):
                    src = rows[:, t, f - 1, :] if f > 0 else dense_rows[:, t, :]
                    last = pe.transpose(bank[:, 128 * k:128 * k + 128], src, ident[:, :])
                last.then_inc(emb_full, 1)

            def lookup(b, i, h):
                if i < EARLY:
                    bank = mlp_bank(("place", i))
                else:
                    bank = emb_bank(("lookup", i, 1))
                if h == 0:
                    if i < EARLY:
                        pe.wait_ge(*mlp_before(b, ("place", i)))
                    else:
                        wait(pe, emb_copied, emb_no(b, ("lookup", i, 1)) - 2)
                    pe.wait_ge(table_low, lookup_no(b, i) + 1)
                for c in range(h * CHUNKS // 2, (h + 1) * CHUNKS // 2):
                    pe.wait_ge(hot_ready, hot_no(b, i, c) + 1)
                    hot = one_hot[0:TROWS, hot_slot(i, c), :]
                    cols = slice(DIM * c, DIM * c + DIM)
                    pe.matmul(bank[:, :], table_h[0:TROWS, i % 2, cols], hot,
                              start=(c == 0), stop=False)
                    last = pe.matmul(bank[:, :], table_l[0:TROWS, i % 2, cols], hot,
                                     start=False, stop=(c == CHUNKS - 1))
                    last.then_inc(hot_used, 1)

            def grams(b, n, part=None):
                if n % 2 == 0:
                    need = [u for u in EMB_USES if u[0] == "lookup" or u[1] == n // 2]
                    pe.wait_ge(emb_copied, emb_no(b, need[-1]) + 1)
                if part != 1:
                    pe.wait_ge(*mix_before(b, ("gram", n)))
                bank = mix_bank(("gram", n))
                for q in (range(HALF) if part is None else range(HALF)[part * HALF // 2:][:HALF // 2]):
                    for j in range(4):
                        s = 4 * (n * HALF + q) + j
                        last = pe.matmul(bank[32 * j:32 * j + SIDE, SIDE * q:SIDE * q + SIDE],
                                         emb[:, s, 1:FEATURES], emb[:, s, 0:SIDE], start=True, stop=True)
                if part != 0:
                    last.then_inc(mix_full, 1)

            def z(b, c, half):
                if half == 0:
                    pe.wait_ge(first_pairs_done, b + 1)
                    pe.wait_ge(*mix_before(b, ("z", c)))
                else:
                    pe.wait_ge(pairs_done, 2 * (b + 1))
                for t in range(TILES)[PAIR_TILES[half]]:
                    last = pe.transpose(mix_bank(("z", c))[0:KCH[c], 128 * t:128 * t + 128],
                                        pairs[:, t, 128 * c:128 * c + KCH[c]], ident[:, :])
                if half == 0:
                    return
                last.then_inc(mix_full, 2 if c == 2 else 1)

            def layer1(b, n, part):
                if part == 0:
                    pe.wait_ge(*mlp_before(b, ("layer1", n)))
                if n == 0 and part == 0:
                    pe.wait_ge(w_low, 2)
                for c in PARTS[part]:
                    k, cols = KCH[c], slice(128 * n, 128 * n + 128)
                    high, low = z_parts(c)
                    bank = mlp_bank(("layer1", n))
                    high_done, low_done = input_done(b, c)
                    pe.wait_ge(*high_done)
                    pe.matmul(bank[:, :], w1h[0:k, c, cols], high, start=(c == 3), stop=False)
                    pe.matmul(bank[:, :], w1l[0:k, c, cols], high, start=False, stop=False)
                    pe.wait_ge(*low_done)
                    last = pe.matmul(bank[:, :], w1h[0:k, c, cols], low,
                                     start=False, stop=(c == 2))
                if part == LAST:
                    last.then_inc(mlp_full, 1)

            def layer2(b, n):
                pe.wait_ge(*mlp_before(b, ("layer2", n)))
                bank = mlp_bank(("layer2", n))
                for c in range(N1):
                    cols = slice(128 * n, 128 * n + 128)
                    pe.wait_ge(*mlp_done(b, ("layer1", c)))
                    pe.matmul(bank[:, :], w2h[:, c, cols], h1h[:, c, :], start=(c == 0), stop=False)
                    pe.matmul(bank[:, :], w2l[:, c, cols], h1h[:, c, :], start=False, stop=False)
                    pe.wait_ge(h1_low, b * N1 + c + 1)
                    last = pe.matmul(bank[:, :], w2h[:, c, cols], h1l[:, c, :],
                                     start=False, stop=(c == N1 - 1))
                last.then_inc(mlp_full, 1)

            def layer3(b):
                pe.wait_ge(*mlp_before(b, ("layer3",)))
                pe.wait_ge(*mlp_done(b, ("layer2", N2 - 1)))
                for c in range(N2):
                    for t in range(TILES):
                        last = pe.matmul(mlp_bank(("layer3",))[32 * t:32 * t + 1, 0:TILE], w3_sb[:, c:c + 1],
                                         h2[:, c, TILE * t:TILE * t + TILE], start=(c == 0), stop=(c == N2 - 1))
                last.then_inc(y_full, 1)

            def block_body(b):
                run(BODY, b, {"gram": grams, "embed": embed}, {"lookup": lookup})
                run(TAIL, b, {"z": z, "layer1": layer1, "layer2": layer2, "layer3": layer3}, ahead)

            ahead = {"lookup": lookup, "embed": embed}
            pe.wait_ge(const_ready, 2)
            run(BODY, -1, {}, {"lookup": lookup})
            run(TAIL, -1, {}, ahead)
            pe.wait_ge(mix_zeroed, 3)
            with pe.Fori(0, BLOCKS - 1) as b:
                block_body(b)
            block_body(BLOCKS - 1)

        @block.scalar
        def _(act):
            def embed(b, t, e):
                act.wait_ge(emb_full, (b * TILES + t) * len(EMBED) + e + 1)
                if (t, e) == (0, 0):
                    wait(act, dense_low, b)
                k = len(EMBED[e])
                act.activation(emb[:, t * TILE:(t + 1) * TILE, EMBED[e][0]:EMBED[e][0] + k],
                               emb_bank(("embed", t, e))[:, 0:128 * k].rearrange("p (k s) -> p s k", k=k),
                               ACT.Copy).then_inc(emb_copied, 1)

            def split_high(b, i):
                act.wait_ge(table_in[i % 2], 16 * slot_uses(b, i))
                wait(act, hot_used, CHUNKS * (slot_before(b, i) + 1))
                act.activation(table_h[0:TROWS, i % 2, :], table[0:TROWS, i % 2, :], ACT.Copy) \
                    .then_inc(table_high, 1)

            def lookup(b, i, h):
                if h == 1 and i >= EARLY:
                    act.wait_ge(hot_used, CHUNKS * (lookup_no(b, i) + 1))
                    act.activation(emb[:, :, ROWED + i], emb_bank(("lookup", i, 1))[:, :], ACT.Copy) \
                        .then_inc(emb_copied, 1)
                if h == 0 and 0 < i < LOOKUPS - 1 and i != EARLY:
                    split_high(b, i + 1)

            def place(b, i):
                wait(act, mix_full, mix_no(b - 1, ("gram", GRAMS - 1)) + 1)
                act.wait_ge(hot_used, CHUNKS * (lookup_no(b, i) + 1))
                act.activation(emb[:, :, ROWED + i], mlp_bank(("place", i))[:, :], ACT.Copy) \
                    .then_inc(mlp_copied, 1)

            def pair(b, k):
                act.wait_ge(turn_done, TILES * b + PAIR_TILES[k].stop)
                for r in range(SIDE if k == 0 else PAIR_ACT):
                    last = act.activation(pairs[:, PAIR_TILES[k], first_pair[r]:first_pair[r] + SIDE - r],
                                          turned[:, PAIR_TILES[k], r, r:SIDE].bitcast(fp32), ACT.Copy)
                last.then_inc((first_pairs_done, pairs_done)[k], 1)

            def z(b, c, half):
                if half == 0:
                    return
                act.wait_ge(mix_full, mix_no(b, ("z", c)) + 1)
                act.wait_ge(pairs_done, 2 * (b + 1))
                act.activation(z_parts(c)[0], mix_bank(("z", c))[0:KCH[c], :], ACT.Copy).then_inc(z_high, 1)

            def dense_part(b):
                act.wait_ge(emb_copied, emb_no(b, ("embed", TILES - 1, 0)) + 1)
                act.activation(as_dense(dense_h[:, :]), dense_columns(), ACT.Copy).then_inc(dense_high, 1)

            def layer1(b, n, part):
                if part == LAST:
                    act.wait_ge(mlp_full, b * (N1 + N2) + n + 1)
                    if n >= 2:
                        act.wait_ge(h1_low, b * N1 + n - 1)
                    act.activation(h1_full[:, n % 2, :], mlp_bank(("layer1", n))[:, :], ACT.Relu,
                                   bias=b1_sb[:, n:n + 1])
                    act.activation(h1h[:, n, :], mlp_bank(("layer1", n))[:, :], ACT.Relu,
                                   bias=b1_sb[:, n:n + 1]).then_inc(mlp_copied, 1)

            def layer2(b, n):
                act.wait_ge(mlp_full, b * (N1 + N2) + N1 + n + 1)
                act.activation(h2[:, n, :], mlp_bank(("layer2", n))[:, :], ACT.Relu,
                               bias=b2_sb[:, n:n + 1]).then_inc(mlp_copied, 1)

            def layer3(b):
                act.wait_ge(y_full, b + 1)
                act.wait_ge(y_out, 16 * (b + 1))
                act.activation(y_rows[:, :].rearrange("o (q j) -> o j q", j=4),
                               mlp_bank(("layer3",))[:, 0:TILE].rearrange("o (j q) -> o j q", j=4),
                               ACT.Copy).then_inc(mlp_copied, 2)
                act.wait_ge(*mlp_done(b, ("layer3",)))
                act.dma_start(out[bass.ds(b * BLOCK, BLOCK), :].rearrange("(t s) o -> t (s o)", t=TILES),
                              y_rows[0:128:32, :]).then_inc(y_out, 16)

            def block_body(b):
                if not isinstance(b, int):
                    split_high(b + 1, 0)
                    split_high(b + 1, 1)
                else:
                    act.wait_ge(*mlp_done(b - 1, ("layer3",)))
                    act.sem_inc(mlp_copied, EARLY)
                run(BODY, b, {"embed": embed, "dense": dense_part, "pair": pair},
                    {"lookup": lookup, "split": split_high})
                run(TAIL, b, {"pair": pair, "z": z, "layer1": layer1, "layer2": layer2, "layer3": layer3},
                    ahead)

            ahead = {"place": place, "lookup": lookup, "embed": embed}
            act.sem_inc(mlp_copied, len(MLP_USES))
            act.sem_inc(y_out, 16)
            split_high(0, 0)
            split_high(0, 1)
            run(BODY, -1, {}, {"lookup": lookup, "split": split_high})
            run(TAIL, -1, {}, ahead)
            act.wait_ge(w1_sum, 2)
            act.activation(w1h[:, :, :], w1_stage[:, 0:4, :], ACT.Copy).then_inc(w_high, 1)
            act.activation(w2h[:, :, :], w2_stage, ACT.Copy).then_inc(w_high, 1)
            with act.Fori(0, BLOCKS - 1) as b:
                block_body(b)
            block_body(BLOCKS - 1)
            act.wait_ge(y_out, 16 * (BLOCKS + 1))

        @block.vector
        def _(dve):
            def split_low(b, i):
                dve.wait_ge(table_high, lookup_no(b, i) + 1)
                wait(dve, hot_used, CHUNKS * (slot_before(b, i) + 1))
                dve.tensor_tensor(table_l[0:TROWS, i % 2, :], table[0:TROWS, i % 2, :],
                                  table_h[0:TROWS, i % 2, :].bitcast(fp32), ALU.subtract) \
                    .then_inc(table_low, 1)

            def hots(b, i, h):
                if h == 0:
                    dve.wait_ge(lids_in[i % 2], 16 * slot_uses(b, i))
                for c in range(h * CHUNKS // 2, (h + 1) * CHUNKS // 2):
                    wait(dve, hot_used, hot_no(b, i, c) + 1 - ONE_HOTS)
                    dve.tensor_scalar(one_hot[0:TROWS, hot_slot(i, c), :], lookup_ids[0:TROWS, i % 2, :],
                                      row_number[0:TROWS, c:c + 1], None, ALU.is_equal) \
                        .then_inc(hot_ready, 1)

            def lookup(b, i, h):
                if i + 1 < LOOKUPS:
                    hots(b, i + 1, h)
                if h == 0 and EARLY < i < LOOKUPS - 1:
                    split_low(b, i + 1)

            def grams(b, n):
                dve.wait_ge(mix_full, mix_no(b, ("gram", n)) + 1)
                dve.tensor_copy(gram[:, :, HALF * n:HALF * n + HALF].rearrange("p r q -> p q r"),
                                mix_bank(("gram", n))[:, 0:SIDE * HALF].rearrange("p (q r) -> p q r", r=SIDE)) \
                    .then_inc(mix_copied, 1)

            def turn(b, t):
                dve.wait_ge(*mix_done(b, ("gram", 2 * t + 1)))
                dve.transpose(turned[:, t, :, :], gram[:, :, 32 * t:32 * t + 32].bitcast(u32)) \
                    .then_inc(turn_done, 1)

            def pair(b, k):
                dve.wait_ge(turn_done, TILES * (b + 1))
                for r in range(PAIR_ACT, SIDE):
                    last = dve.tensor_copy(pairs[:, PAIR_TILES[k], first_pair[r]:first_pair[r] + SIDE - r],
                                           turned[:, PAIR_TILES[k], r, r:SIDE].bitcast(fp32))
                last.then_inc(pairs_done, 1)

            def z(b, c, half):
                if half == 0:
                    return
                dve.wait_ge(z_high, z_no(b, c) + 1)
                (high, low), src = z_parts(c), mix_bank(("z", c))[0:KCH[c], :]
                dve.tensor_tensor(low, src, high.bitcast(fp32), ALU.subtract) \
                    .then_inc(mix_copied, 2 if c == 2 else 1)

            def dense_part(b):
                dve.wait_ge(dense_high, b + 1)
                dve.tensor_tensor(as_dense(dense_l[:, :]), dense_columns(),
                                  as_dense(dense_h[:, :]).bitcast(fp32), ALU.subtract).then_inc(dense_low, 1)

            def layer1(b, n, part):
                if part == LAST:
                    dve.wait_ge(*mlp_done(b, ("layer1", n)))
                    dve.tensor_tensor(h1l[:, n, :], h1_full[:, n % 2, :], h1h[:, n, :].bitcast(fp32),
                                      ALU.subtract).then_inc(h1_low, 1)

            def block_body(b):
                for n in range(GRAMS):
                    if n == 5:
                        dense_part(b)
                    grams(b, n)
                    if n % 2 == 1:
                        turn(b, n // 2)
                    if not isinstance(b, int):
                        for step, *m in begin[n]:
                            step(b + 1, *m)
                run(TAIL, b, {"pair": pair, "z": z, "layer1": layer1}, {"lookup": lookup})

            begin = [[(split_low, 0), (hots, 0, 0)], [(split_low, 1), (hots, 0, 1)], [], [],
                     [(hots, 1, 0), (hots, 1, 1), (hots, 2, 0), (split_low, 2), (hots, 2, 1)], [],
                     [(split_low, 3)], []]
            dve.memset(w1_stage[:, 2, :], 0.0).then_inc(w1_sum, 1)
            for bank in mix_ps:
                dve.memset(bank[:, :], 0.0).then_inc(mix_zeroed, 1)
            dve.sem_inc(mix_copied, len(MIX_USES))
            dve.wait_ge(const_ready, 2)
            for steps in begin:
                for step, *m in steps:
                    step(0, *m)
            run(TAIL, -1, {}, {"lookup": lookup})
            dve.wait_ge(weights_in, 16 * 9)
            dve.tensor_tensor(w1_stage[:, 3, :], w1_stage[:, 3, :], w1_stage[:, 4, :], ALU.add) \
                .then_inc(w1_sum, 1)
            dve.wait_ge(w_high, 2)
            dve.tensor_tensor(w1l[:, :, :], w1_stage[:, 0:4, :], w1h[:, :, :].bitcast(fp32), ALU.subtract) \
                .then_inc(w_low, 1)
            dve.tensor_tensor(w2l[:, :, :], w2_stage, w2h[:, :, :].bitcast(fp32), ALU.subtract) \
                .then_inc(w_low, 1)
            dve.wait_ge(w_low, 2)
            with dve.Fori(0, BLOCKS - 1) as b:
                block_body(b)
            block_body(BLOCKS - 1)


def kernel(**inputs):
    import concourse.bacc as bacc
    from concourse.bass_utils import run_bass_kernel_spmd

    ids = np.asarray(inputs["ids"])
    w1 = np.asarray(inputs["W_top1"])
    arrays = {
        "dense": np.ascontiguousarray(inputs["r_dense_features"]),
        "ids_gathered": np.ascontiguousarray(ids[:, GATHERED]),
        "ids_looked_up": np.ascontiguousarray(ids[:, LOOKED_UP].T),
        "w1_dense": np.ascontiguousarray(np.concatenate([w1[:DIM], w1[DIM + PAIRS:]])),
        "w1_pairs": np.ascontiguousarray(w1[pair_rows()]),
        "b1": np.ascontiguousarray(np.asarray(inputs["b_top1"]).reshape(-1, 128).T),
        "w2": np.ascontiguousarray(inputs["W_top2"]),
        "b2": np.ascontiguousarray(np.asarray(inputs["b_top2"]).reshape(-1, 128).T),
        "w3": np.ascontiguousarray(np.asarray(inputs["W_top3"]).reshape(-1, 128).T),
    }
    for t in range(TABLES):
        arrays[f"table{t}"] = np.ascontiguousarray(inputs[f"tbl_{t}"])

    nc = bacc.Bacc("TRN2", target_bir_lowering=False, num_devices=1)
    ap = {name: nc.dram_tensor(name, a.shape, mybir.dt.from_np(a.dtype), kind="ExternalInput").ap()
          for name, a in arrays.items()}
    out = nc.dram_tensor("y", (BATCH, 1), mybir.dt.float32, kind="ExternalOutput").ap()
    dlrm_tower(nc, ap["dense"], ap["ids_gathered"], ap["ids_looked_up"],
               [ap[f"table{t}"] for t in range(TABLES)], ap["w1_dense"], ap["w1_pairs"],
               ap["b1"], ap["w2"], ap["b2"], ap["w3"], out)
    return run_bass_kernel_spmd(nc, [arrays], core_ids=[0]).results[0]["y"]
```
